# Optimizing a Trainium2 kernel written in Bass

```python
import numpy as np
import jax
import jax.numpy as jnp

def _softmax(x, axis=-1):
    return jax.nn.softmax(x, axis=axis)

def _gelu(x):
    return jax.nn.gelu(x, approximate=True)

def _silu(x):
    return jax.nn.silu(x)

def _sigmoid(x):
    return jax.nn.sigmoid(x)

def _layernorm(x, axis=-1, eps=1e-05):
    m = jnp.mean(x, axis=axis, keepdims=True)
    v = jnp.var(x, axis=axis, keepdims=True)
    return (x - m) / jnp.sqrt(v + eps)

def _scatter_add(tgt, idx, src, axis=0):
    return tgt.at[idx].add(src)

def _segment_sum(src, seg, n):
    return jax.ops.segment_sum(src, seg, n)
kernel_name = 'mk_gnn_preln_d2_gnn_r16_b1b9ad'

def setup_inputs(seed: int=0):
    np.random.seed(seed)
    _w = jnp.asarray

    def _rec_inputs():
        import jax
        import jax.numpy as jnp
        _gk = jax.random.key(seed)
        x = -0.0005121 + 1.001 * jax.random.normal(jax.random.fold_in(_gk, 1), (6250, 160), jnp.float32)
        src = jax.random.randint(jax.random.fold_in(_gk, 2), (200000,), 0, 6250, jnp.int32)
        dst = jnp.minimum((6250 * jax.random.uniform(jax.random.fold_in(_gk, 3), (200000,)) ** 2.0).astype(jnp.int32), 99999)
        _o = jnp.argsort(dst, stable=True)
        src = src[_o]
        dst = dst[_o]
        edge_attr_16 = jax.random.uniform(jax.random.fold_in(_gk, 12), (200000, 16), jnp.float32, 0.0, 1)
        edge_attr_4 = 0.000898722 + 1.00012 * jax.random.normal(jax.random.fold_in(_gk, 13), (200000, 4), jnp.float32)
        node_vec1 = jax.random.uniform(jax.random.fold_in(_gk, 15), (6250, 1), jnp.float32, 0.0, 1)
        return (x, src, dst, edge_attr_16, edge_attr_4, node_vec1)
    x, src, dst, edge_attr_16, edge_attr_4, node_vec1 = _rec_inputs()

    def _L0_gnn_setup():
        import jax, jax.numpy as jnp
        import numpy as np
        N, E = (1250, 20000)
        CS, CV = (64, 32)
        AS_, AV, H = (16, 8, 4)
        NB = 16
        SQRT3 = 1.7320508075688772
        SQRT2 = 1.4142135623730951
        EPS = 1e-05

        def _cg_tp(s, v, y0, y1, w_ss, w_sv, w_vs, w_vv0, w_vv1):
            out_s = jnp.concatenate([w_ss * s * y0[:, None], w_vv0 * (jnp.einsum('eci,ei->ec', v, y1) / SQRT3)], axis=-1)
            out_v = jnp.concatenate([(w_sv * s)[:, :, None] * y1[:, None, :], (w_vs * jnp.ones_like(v[..., 0]))[..., None] * v * y0[:, None, None], (w_vv1 * jnp.ones_like(v[..., 0]))[..., None] * (jnp.cross(v, y1[:, None, :]) / SQRT2)], axis=1)
            return (out_s, out_v)

        def _equiv_layernorm(s, v, gamma_s, beta_s, gamma_v):
            mu = jnp.mean(s, axis=-1, keepdims=True)
            var = jnp.var(s, axis=-1, keepdims=True)
            s_n = (s - mu) * jax.lax.rsqrt(var + EPS) * gamma_s + beta_s
            rms = jnp.sqrt(jnp.mean(jnp.sum(v * v, axis=-1), axis=-1, keepdims=True) + EPS)
            v_n = v / rms[..., None] * gamma_v[None, :, None]
            return (s_n, v_n)
        key = jax.random.key(seed)
        ks = jax.random.split(key, 26)

        def rn(k, shape, fan):
            return jax.random.normal(k, shape, jnp.float32) / np.sqrt(fan)
        D1S, D1V = (CS + CV, CS + 2 * CV)
        WN = 2 * CS + 3 * CV
        inp = {'node': jax.random.normal(ks[0], (N, CS + 3 * CV), jnp.float32), 'edge_index': jax.random.randint(ks[1], (2, E), 0, N, jnp.int64 if jax.config.jax_enable_x64 else jnp.int32), 'rbf': jax.random.uniform(ks[2], (E, NB), jnp.float32), 'rsh': jax.random.normal(ks[3], (E, 4), jnp.float32), 'gamma_s': jnp.ones((CS,), jnp.float32), 'beta_s': jnp.zeros((CS,), jnp.float32), 'gamma_v': jnp.ones((CV,), jnp.float32), 'Ws_src': rn(ks[4], (CS, CS), CS), 'Wv_src': rn(ks[5], (CV, CV), CV), 'Ws_dst': rn(ks[6], (CS, CS), CS), 'Wv_dst': rn(ks[7], (CV, CV), CV), 'W_rbf': rn(ks[8], (NB, WN), NB), 'W_alpha': rn(ks[9], (D1S, H * AS_), D1S), 'alpha_dot': rn(ks[10], (1, H, AS_), AS_), 'Ws_val': rn(ks[11], (D1S, CS), D1S), 'Wv_val': rn(ks[12], (D1V, CV), D1V), 'Wg': rn(ks[13], (CS, CV), CS), 'w2_ss': rn(ks[14], (CS,), 1), 'w2_sv': rn(ks[15], (CS,), 1), 'w2_vs': rn(ks[16], (CV,), 1), 'w2_vv0': rn(ks[17], (CV,), 1), 'w2_vv1': rn(ks[18], (CV,), 1), 'Ws_vlin': rn(ks[19], (D1S, H * AS_), D1S), 'Wv_vlin': rn(ks[20], (D1V, H * AV), D1V), 'Wps': rn(ks[21], (H * AS_, CS), H * AS_), 'Wpv': rn(ks[22], (H * AV, CV), H * AV)}
        return inp
    _L0_gnn_all = _L0_gnn_setup()
    _L0_gnn_in = {k: v for k, v in _L0_gnn_all.items() if k in ('gamma_s', 'beta_s', 'gamma_v', 'Ws_src', 'Wv_src', 'Ws_dst', 'Wv_dst', 'W_rbf', 'W_alpha', 'alpha_dot', 'Ws_val', 'Wv_val', 'Wg', 'w2_ss', 'w2_sv', 'w2_vs', 'w2_vv0', 'w2_vv1', 'Ws_vlin', 'Wv_vlin', 'Wps', 'Wpv')}
    del _L0_gnn_all

    def _L1_gnn_setup():
        import jax, jax.numpy as jnp
        import numpy as np
        N = 1250
        E = 20000
        MUL0 = 64
        MUL1 = 32
        FC_IN = 16
        FC_H = 64
        WNUM = 192
        key = jax.random.key(seed)
        ks = jax.random.split(key, 16)
        return {'x': jax.random.normal(ks[0], (N, MUL0 + 3 * MUL1), jnp.float32), 'node_attr': jnp.ones((N, 1), jnp.float32), 'edge_scalars': jax.random.normal(ks[1], (E, FC_IN), jnp.float32), 'edge_attr_sh': jax.random.normal(ks[2], (E, 4), jnp.float32), 'edge_src': jax.random.randint(ks[3], (E,), 0, N), 'edge_dst': jax.random.randint(ks[4], (E,), 0, N), 'Wfc1': jax.random.normal(ks[5], (FC_IN, FC_H), jnp.float32), 'Wfc2': jax.random.normal(ks[6], (FC_H, WNUM), jnp.float32), 'Wsc0': jax.random.normal(ks[7], (MUL0, MUL0), jnp.float32), 'Wsc1': jax.random.normal(ks[8], (MUL1, MUL1), jnp.float32), 'Wl1_0': jax.random.normal(ks[9], (MUL0, MUL0), jnp.float32), 'Wl1_1': jax.random.normal(ks[10], (MUL1, MUL1), jnp.float32), 'Wl2_s': jax.random.normal(ks[11], (MUL0 + MUL1, MUL0), jnp.float32), 'Wl2_v': jax.random.normal(ks[12], (MUL0 + MUL1, MUL1), jnp.float32), 'Wa': 0.1 * jax.random.normal(ks[13], (MUL0 + MUL1, 1), jnp.float32)}
    _L1_gnn_all = _L1_gnn_setup()
    _L1_gnn_in = {k: v for k, v in _L1_gnn_all.items() if k in ('Wfc1', 'Wfc2', 'Wsc0', 'Wsc1', 'Wl1_0', 'Wl1_1', 'Wl2_s', 'Wl2_v', 'Wa')}
    del _L1_gnn_all
    return {'x': x, 'src': src, 'dst': dst, 'edge_attr_16': edge_attr_16, 'edge_attr_4': edge_attr_4, 'node_vec1': node_vec1, 'L0_gnn_gamma_s': _L0_gnn_in['gamma_s'], 'L0_gnn_beta_s': _L0_gnn_in['beta_s'], 'L0_gnn_gamma_v': _L0_gnn_in['gamma_v'], 'L0_gnn_Ws_src': _L0_gnn_in['Ws_src'], 'L0_gnn_Wv_src': _L0_gnn_in['Wv_src'], 'L0_gnn_Ws_dst': _L0_gnn_in['Ws_dst'], 'L0_gnn_Wv_dst': _L0_gnn_in['Wv_dst'], 'L0_gnn_W_rbf': _L0_gnn_in['W_rbf'], 'L0_gnn_W_alpha': _L0_gnn_in['W_alpha'], 'L0_gnn_alpha_dot': _L0_gnn_in['alpha_dot'], 'L0_gnn_Ws_val': _L0_gnn_in['Ws_val'], 'L0_gnn_Wv_val': _L0_gnn_in['Wv_val'], 'L0_gnn_Wg': _L0_gnn_in['Wg'], 'L0_gnn_w2_ss': _L0_gnn_in['w2_ss'], 'L0_gnn_w2_sv': _L0_gnn_in['w2_sv'], 'L0_gnn_w2_vs': _L0_gnn_in['w2_vs'], 'L0_gnn_w2_vv0': _L0_gnn_in['w2_vv0'], 'L0_gnn_w2_vv1': _L0_gnn_in['w2_vv1'], 'L0_gnn_Ws_vlin': _L0_gnn_in['Ws_vlin'], 'L0_gnn_Wv_vlin': _L0_gnn_in['Wv_vlin'], 'L0_gnn_Wps': _L0_gnn_in['Wps'], 'L0_gnn_Wpv': _L0_gnn_in['Wpv'], 'L1_gnn_Wfc1': _L1_gnn_in['Wfc1'], 'L1_gnn_Wfc2': _L1_gnn_in['Wfc2'], 'L1_gnn_Wsc0': _L1_gnn_in['Wsc0'], 'L1_gnn_Wsc1': _L1_gnn_in['Wsc1'], 'L1_gnn_Wl1_0': _L1_gnn_in['Wl1_0'], 'L1_gnn_Wl1_1': _L1_gnn_in['Wl1_1'], 'L1_gnn_Wl2_s': _L1_gnn_in['Wl2_s'], 'L1_gnn_Wl2_v': _L1_gnn_in['Wl2_v'], 'L1_gnn_Wa': _L1_gnn_in['Wa']}

def reference(x, src, dst, edge_attr_16, edge_attr_4, node_vec1, L0_gnn_gamma_s, L0_gnn_beta_s, L0_gnn_gamma_v, L0_gnn_Ws_src, L0_gnn_Wv_src, L0_gnn_Ws_dst, L0_gnn_Wv_dst, L0_gnn_W_rbf, L0_gnn_W_alpha, L0_gnn_alpha_dot, L0_gnn_Ws_val, L0_gnn_Wv_val, L0_gnn_Wg, L0_gnn_w2_ss, L0_gnn_w2_sv, L0_gnn_w2_vs, L0_gnn_w2_vv0, L0_gnn_w2_vv1, L0_gnn_Ws_vlin, L0_gnn_Wv_vlin, L0_gnn_Wps, L0_gnn_Wpv, L1_gnn_Wfc1, L1_gnn_Wfc2, L1_gnn_Wsc0, L1_gnn_Wsc1, L1_gnn_Wl1_0, L1_gnn_Wl1_1, L1_gnn_Wl2_s, L1_gnn_Wl2_v, L1_gnn_Wa):
    import jax
    import jax.numpy as jnp

    def _L0_gnn_ref(node, rbf, rsh, gamma_s, beta_s, gamma_v, Ws_src, Wv_src, Ws_dst, Wv_dst, W_rbf, W_alpha, alpha_dot, Ws_val, Wv_val, Wg, w2_ss, w2_sv, w2_vs, w2_vv0, w2_vv1, Ws_vlin, Wv_vlin, Wps, Wpv, edge_index):
        import jax, jax.numpy as jnp
        import numpy as np
        N, E = (1250, 20000)
        CS, CV = (64, 32)
        AS_, AV, H = (16, 8, 4)
        NB = 16
        SQRT3 = 1.7320508075688772
        SQRT2 = 1.4142135623730951
        EPS = 1e-05

        def _cg_tp(s, v, y0, y1, w_ss, w_sv, w_vs, w_vv0, w_vv1):
            out_s = jnp.concatenate([w_ss * s * y0[:, None], w_vv0 * (jnp.einsum('eci,ei->ec', v, y1) / SQRT3)], axis=-1)
            out_v = jnp.concatenate([(w_sv * s)[:, :, None] * y1[:, None, :], (w_vs * jnp.ones_like(v[..., 0]))[..., None] * v * y0[:, None, None], (w_vv1 * jnp.ones_like(v[..., 0]))[..., None] * (jnp.cross(v, y1[:, None, :]) / SQRT2)], axis=1)
            return (out_s, out_v)

        def _equiv_layernorm(s, v, gamma_s, beta_s, gamma_v):
            mu = jnp.mean(s, axis=-1, keepdims=True)
            var = jnp.var(s, axis=-1, keepdims=True)
            s_n = (s - mu) * jax.lax.rsqrt(var + EPS) * gamma_s + beta_s
            rms = jnp.sqrt(jnp.mean(jnp.sum(v * v, axis=-1), axis=-1, keepdims=True) + EPS)
            v_n = v / rms[..., None] * gamma_v[None, :, None]
            return (s_n, v_n)
        n = node.shape[0]
        e = rsh.shape[0]
        s = node[:, :CS]
        v = node[:, CS:].reshape(n, CV, 3)
        s_n, v_n = _equiv_layernorm(s, v, gamma_s, beta_s, gamma_v)
        src, dst = (edge_index[0], edge_index[1])
        msg_s = (s_n @ Ws_src)[src] + (s_n @ Ws_dst)[dst]
        msg_v = jnp.einsum('ncx,cd->ndx', v_n, Wv_src)[src] + jnp.einsum('ncx,cd->ndx', v_n, Wv_dst)[dst]
        y0, y1 = (rsh[:, 0], rsh[:, 1:4])
        w1 = rbf @ W_rbf
        m1_s, m1_v = _cg_tp(msg_s, msg_v, y0, y1, w1[:, :CS], w1[:, CS:2 * CS], w1[:, 2 * CS:2 * CS + CV], w1[:, 2 * CS + CV:2 * CS + 2 * CV], w1[:, 2 * CS + 2 * CV:])
        a = (m1_s @ W_alpha).reshape(e, H, AS_)
        a = jnp.where(a > 0, a, 0.2 * a)
        a = jnp.sum(a * alpha_dot, axis=-1, keepdims=True)
        amax = jax.ops.segment_max(a, dst, num_segments=n)
        amax = jnp.where(jnp.isfinite(amax), amax, 0.0)
        ex = jnp.exp(a - amax[dst])
        den = jax.ops.segment_sum(ex, dst, num_segments=n)
        alpha = ex / (den[dst] + 1e-16)
        val_s = m1_s @ Ws_val
        val_v = jnp.einsum('ecx,cd->edx', m1_v, Wv_val)
        val_v = val_v * jax.nn.sigmoid(val_s @ Wg)[..., None]
        val_s = jax.nn.sigmoid(val_s)
        m2_s, m2_v = _cg_tp(val_s, val_v, y0, y1, w2_ss, w2_sv, w2_vs, w2_vv0, w2_vv1)
        hs = (m2_s @ Ws_vlin).reshape(e, H, AS_)
        hv = jnp.einsum('ecx,cd->edx', m2_v, Wv_vlin).reshape(e, H, AV, 3)
        h = jnp.concatenate([hs, hv.reshape(e, H, AV * 3)], axis=-1)
        agg = jax.ops.segment_sum(alpha * h, dst, num_segments=n)
        agg_s = agg[:, :, :AS_].reshape(n, H * AS_)
        agg_v = agg[:, :, AS_:].reshape(n, H * AV, 3)
        out = node + jnp.concatenate([agg_s @ Wps, jnp.einsum('ncx,cd->ndx', agg_v, Wpv).reshape(n, CV * 3)], axis=-1)
        return out

    def _L1_gnn_ref(x, node_attr, edge_scalars, edge_attr_sh, edge_src, edge_dst, Wfc1, Wfc2, Wsc0, Wsc1, Wl1_0, Wl1_1, Wl2_s, Wl2_v, Wa):
        import jax, jax.numpy as jnp
        import numpy as np
        N = 1250
        E = 20000
        MUL0 = 64
        MUL1 = 32
        FC_IN = 16
        FC_H = 64
        WNUM = 192
        n = x.shape[0]
        x0 = x[:, :MUL0]
        x1 = x[:, MUL0:].reshape(n, MUL1, 3)
        a = node_attr
        h = jax.nn.silu(edge_scalars @ (Wfc1 / jnp.sqrt(jnp.float32(FC_IN))))
        w = h @ (Wfc2 / jnp.sqrt(jnp.float32(FC_H)))
        w0 = w[:, :64]
        w1 = w[:, 64:128]
        w2 = w[:, 128:160]
        w3 = w[:, 160:192]
        inv8 = 1.0 / jnp.sqrt(jnp.float32(MUL0))
        inv32 = 1.0 / jnp.sqrt(jnp.float32(MUL1))
        sc = jnp.concatenate([x0 @ Wsc0 * a * inv8, (jnp.einsum('num,uv->nvm', x1, Wsc1) * a[..., None] * inv32).reshape(n, 3 * MUL1)], axis=1)
        f0 = x0 @ Wl1_0 * a * inv8
        f1 = jnp.einsum('num,uv->nvm', x1, Wl1_1) * a[..., None] * inv32
        e0 = f0[edge_src]
        e1 = f1[edge_src]
        sh0 = edge_attr_sh[:, :1]
        sh1 = edge_attr_sh[:, 1:4]
        mid0 = w0 * e0 * sh0
        mid1 = w3 * jnp.einsum('eum,em->eu', e1, sh1) / jnp.sqrt(3.0)
        mid2 = w1[:, :, None] * e0[:, :, None] * sh1[:, None, :]
        mid3 = w2[:, :, None] * e1 * sh0[:, :, None]
        cnt = jnp.clip(jax.ops.segment_sum(jnp.ones(edge_dst.shape, x.dtype), edge_dst, num_segments=n), 1.0)

        def smean(v):
            s = jax.ops.segment_sum(v, edge_dst, num_segments=n)
            return s / cnt.reshape((n,) + (1,) * (v.ndim - 1))
        n0, n1 = (smean(mid0), smean(mid1))
        n2, n3 = (smean(mid2), smean(mid3))
        scal = jnp.concatenate([n0, n1], axis=1)
        vec = jnp.concatenate([n2, n3], axis=1)
        inv96 = 1.0 / jnp.sqrt(jnp.float32(MUL0 + MUL1))
        alpha = scal @ Wa * a * inv96
        out_s = scal @ Wl2_s * a * inv96
        out_v = jnp.einsum('num,uv->nvm', vec, Wl2_v) * a[..., None] * inv96
        conv = jnp.concatenate([out_s, out_v.reshape(n, 3 * MUL1)], axis=1)
        return sc + alpha * conv
    edge_index = jnp.stack([src, dst])
    h = jnp.maximum(_layernorm(x, axis=-1), 0.0)
    x = x + _L0_gnn_ref(h, edge_attr_16, edge_attr_4, L0_gnn_gamma_s, L0_gnn_beta_s, L0_gnn_gamma_v, L0_gnn_Ws_src, L0_gnn_Wv_src, L0_gnn_Ws_dst, L0_gnn_Wv_dst, L0_gnn_W_rbf, L0_gnn_W_alpha, L0_gnn_alpha_dot, L0_gnn_Ws_val, L0_gnn_Wv_val, L0_gnn_Wg, L0_gnn_w2_ss, L0_gnn_w2_sv, L0_gnn_w2_vs, L0_gnn_w2_vv0, L0_gnn_w2_vv1, L0_gnn_Ws_vlin, L0_gnn_Wv_vlin, L0_gnn_Wps, L0_gnn_Wpv, edge_index)
    h = jnp.maximum(_layernorm(x, axis=-1), 0.0)
    x = x + _L1_gnn_ref(h, node_vec1, edge_attr_16, edge_attr_4, src, dst, L1_gnn_Wfc1, L1_gnn_Wfc2, L1_gnn_Wsc0, L1_gnn_Wsc1, L1_gnn_Wl1_0, L1_gnn_Wl1_1, L1_gnn_Wl2_s, L1_gnn_Wl2_v, L1_gnn_Wa)
    return x

_drawn_inputs = setup_inputs


def setup_inputs(seed=0):
    import zlib

    import numpy as np

    out = dict(_drawn_inputs(seed))
    spreads = {'L0_gnn_gamma_s': (1.0, 0.6), 'L0_gnn_beta_s': (0.0, 0.8), 'L0_gnn_gamma_v': (1.0, 0.6)}
    factors = {'L0_gnn_w2_vv1': 2.802,
     'L1_gnn_Wfc1': 8.0,
     'L1_gnn_Wfc2': 8.0,
     'L1_gnn_Wl1_0': 8.0,
     'L1_gnn_Wl1_1': 8.0,
     'L1_gnn_Wl2_s': 8.0,
     'L1_gnn_Wl2_v': 8.0,
     'L1_gnn_Wa': 8.0,
     'L1_gnn_Wsc0': 64.0,
     'L1_gnn_Wsc1': 64.0}
    for name, (base, spread) in spreads.items():
        noise = np.random.default_rng([zlib.crc32(name.encode()), seed]).standard_normal(out[name].shape)
        drawn = base * np.exp(spread * noise) if base else spread * noise
        out[name] = jnp.asarray(drawn.astype(out[name].dtype))
    for name, factor in factors.items():
        out[name] = (out[name] * factor).astype(out[name].dtype)
    return out
```

```python
import math
from contextlib import ExitStack

import numpy as np
import concourse.bass as bass
from concourse import mybir

F32 = mybir.dt.float32
I32 = mybir.dt.int32
ALU = mybir.AluOpType
ACT = mybir.ActivationFunctionType
AX = mybir.AxisListType

P = 128
N_NODES, N_EDGES = 6250, 200000
CS, CV, NB, HEADS, AS, AV = 64, 32, 16, 4, 16, 8
D = CS + 3 * CV
TILES = 4
GE = TILES * P
NG = -(-N_EDGES // GE)
NG_PAD = 392
GROUP_ROWS = 98
NT = -(-N_NODES // P)
CH = 7
NCH = NT // CH
NODES_PAD = NT * P
STATE_ROWS = 50 * P
HW = 1 + AS + 3 * AV
SW = HEADS * (1 + HW)
QW = CS + 1 + 3 * CV + 1
LEAST = -1e30
EPS = 1e-5
R2, R3 = 1 / math.sqrt(2.0), 1 / math.sqrt(3.0)
MAX_W = 50 * NG_PAD


class Chain:

    def __init__(self, eng, sem, per_round):
        self.eng, self.sem, self.per, self.base, self.k = eng, sem, per_round, 0, 0

    def begin(self, round_):
        self.base, self.k = round_ * self.per, 0

    def end(self):
        assert self.k == self.per, self.k

    def step(self, instruction):
        self.k += 1
        instruction.then_inc(self.sem, 1)
        self.eng.wait_ge(self.sem, self.base + self.k)


def wait_apart(eng, sem, value, tick):
    eng.wait_ge(sem, value)
    eng.sem_inc(tick, 1)


def build(nc, ins, out):
    ctx = ExitStack()
    with ctx:
        ctx.enter_context(nc.allow_non_contiguous_dma(reason="small tables, once"))
        program(nc, ctx, ins, out)


def program(nc, ctx, A, out):
    def sb(name, shape, dt=F32):
        return ctx.enter_context(nc.sbuf_tensor(name, shape, dt))

    def sem(name):
        return ctx.enter_context(nc.semaphore(name))

    def dram(name, shape, dt=F32):
        return nc.dram_tensor(name, shape, dt, kind="Internal").ap()

    src_tab = dram("src_tab", (NODES_PAD, D))
    dst_tab = dram("dst_tab", (NODES_PAD, D))
    f_tab = dram("f_tab", (NODES_PAD, D))
    state = dram("state", (STATE_ROWS, SW))
    sums = dram("sums", (STATE_ROWS, QW))
    group_dram = dram("group_dram", (2, NG_PAD))

    ident = sb("ident", [P, P])
    iota_row = sb("iota_row", [P, P])
    iota_col = sb("iota_col", [P, 1])
    least_bc = sb("least_bc", [P, NG_PAD])
    window_from = sb("window_from", [1, NG_PAD + 8], I32)
    least_i = sb("least_i", [1, NG_PAD], I32)
    idx_all = sb("idx_all", [P, NG_PAD, 2 * TILES], I32)
    keep = sb("keep", [P, NT, D])
    w_edge = sb("w_edge", [64, 6, P])
    w_msg = sb("w_msg", [P, 6, 256])
    w_val = sb("w_val", [P, 5, D])
    adot = sb("adot", [P, HEADS * AS])
    gam_s = sb("gam_s", [P, CS])
    bet_s = sb("bet_s", [P, CS])
    gam_v = sb("gam_v", [P, CV])
    w_n0s = sb("w_n0s", [64, 2 * CS])
    w_n0v = sb("w_n0v", [96, 6 * CV])
    w_n1s = sb("w_n1s", [64, 2 * CS])
    w_n1v = sb("w_n1v", [96, 6 * CV])
    w_out_a = sb("w_out_a", [P, D])
    w_out_b = sb("w_out_b", [CV, D])
    w_fc1 = sb("w_fc1", [NB, 64])
    w_f01 = sb("w_f01", [64, P])
    w_f3 = sb("w_f3", [64, 96])
    w_f2 = sb("w_f2", [64, 96])
    w_c1 = sb("w_c1", [P, 97])
    w_c2 = sb("w_c2", [96, 65])
    w_c3 = sb("w_c3", [96, 96])
    attr = sb("attr", [P, NT])

    psum = [ctx.enter_context(nc.psum_tensor(f"bank_pair_{i}", [P, 1024], F32)) for i in range(4)]

    def heads(ap):
        return ap.rearrange("p (h c) -> p h c", h=HEADS)

    with ExitStack() as sx:
        def tmp(name, shape, dt=F32):
            return sx.enter_context(nc.sbuf_tensor(name, shape, dt))

        s_zero, s_load, s_ident, s_scale, s_gate, s_gatec = (sem(n) for n in (
            "s_zero", "s_load", "s_ident", "s_scale", "s_gate", "s_gatec"))
        s_dst, s_ext, s_extw, s_row, s_sc, s_init, s_initd, s_meta = (sem(n) for n in (
            "s_dst", "s_ext", "s_extw", "s_row", "s_sc", "s_init", "s_initd", "s_meta"))
        val_t = tmp("val_t", [CS, CS + 3 * CV])
        wg = tmp("wg", [CS, CV])
        scale5 = tmp("scale5", [P, 5])
        fac5 = tmp("fac5", [P, 5])
        dst_g = tmp("dst_g", [GROUP_ROWS, NG_PAD // GROUP_ROWS, GE], I32)
        ext_i = tmp("ext_i", [GROUP_ROWS, 2, NG_PAD // GROUP_ROWS])
        row = tmp("row", [1, 2, NG_PAD])
        cnt_f = tmp("cnt_f", [1, NG_PAD])
        cnt_i = tmp("cnt_i", [1, NG_PAD], I32)
        scan_a = tmp("scan_a", [1, NG_PAD])
        scan_b = tmp("scan_b", [1, NG_PAD])
        init_state = tmp("init_state", [P, 10, SW])
        iota_i = tmp("iota_i", [P, P], I32)
        iota_ci = tmp("iota_ci", [P, 1], I32)
        n_load = [0]

        with nc.Block() as block:
            @block.sync
            def _(sp):
                sp.dma_start(dst_g[:], A["dst_rows"].rearrange("(c p) e -> p c e", p=GROUP_ROWS)).then_inc(s_dst, 16)
                sp.wait_ge(s_zero, 1)

                def put(to, frm):
                    sp.dma_start(to, frm).then_inc(s_load, 16)
                    n_load[0] += 16

                put(idx_all[:], A["idx"].rearrange("g p c -> p g c"))
                put(adot[:], A["alpha_dot"].partition_broadcast(P))
                put(gam_s[:], A["gamma_s"].partition_broadcast(P))
                put(bet_s[:], A["beta_s"].partition_broadcast(P))
                put(gam_v[:], A["gamma_v"].partition_broadcast(P))
                put(attr[:], A["node_attr"])
                Wr = A["W_rbf"]
                o_ss, o_sv, o_vs, o_vv0, o_vv1 = 0, CS, 2 * CS, 2 * CS + CV, 2 * CS + 2 * CV

                def edge_rows(k):
                    return slice(NB * k, NB * k + NB)

                put(w_edge[edge_rows(0), 0, 0:64], Wr[:, o_ss:o_ss + 64])
                put(w_edge[edge_rows(1), 0, 64:128], Wr[:, o_sv:o_sv + 64])
                put(w_edge[edge_rows(2), 1, 0:64], Wr[:, o_sv:o_sv + 64])
                put(w_edge[edge_rows(3), 1, 64:128], Wr[:, o_sv:o_sv + 64])
                for j in range(3):
                    c = slice(32 * j, 32 * j + 32)
                    put(w_edge[edge_rows(j + 1), 2, c], Wr[:, o_vv0:o_vv0 + 32])
                    put(w_edge[edge_rows(0), 3, c], Wr[:, o_vs:o_vs + 32])
                    put(w_edge[edge_rows((j + 1) % 3 + 1), 4, c], Wr[:, o_vv1:o_vv1 + 32])
                    put(w_edge[edge_rows((j + 2) % 3 + 1), 5, c], Wr[:, o_vv1:o_vv1 + 32])
                Wa, Ws, Wv = A["W_alpha"], A["Ws_val"], A["Wv_val"]
                put(w_msg[0:64, 0, 96:160], Ws[0:64, :])
                put(w_msg[0:64, 0, 192:256], Wa[0:64, :])
                put(w_msg[64:128, 0, 0:32], Wv[0:64, :])
                put(w_msg[0:64, 1, 32:64], Wv[0:64, :])
                put(w_msg[64:128, 1, 64:96], Wv[0:64, :])
                for j in range(3):
                    r = slice(32 * j, 32 * j + 32)
                    u, w = 32 * ((j + 2) % 3), 32 * ((j + 1) % 3)
                    put(w_msg[r, 2, 96:160], Ws[64:96, :])
                    put(w_msg[r, 2, 192:256], Wa[64:96, :])
                    put(w_msg[r, 3, r], Wv[64:96, :])
                    put(w_msg[r, 4, u:u + 32], Wv[96:128, :])
                    put(w_msg[r, 5, w:w + 32], Wv[96:128, :])
                put(val_t[:, 0:64], A["Ws_val_t"][:, 0:64])
                for j in range(3):
                    put(val_t[:, 64 + 32 * j:96 + 32 * j], A["Ws_val_t"][:, 64:96])
                put(wg[:], A["Wg"])
                for b, r, _, source, first, axis, vec, vfirst in value_pieces():
                    to = heads(w_val[r:r + 32, b, :])
                    frm = A[source][first:first + 32, :]
                    if axis is None:
                        put(to[:, :, 0:AS], frm.rearrange("p (h c) -> p h c", h=HEADS))
                    else:
                        put(to[:, :, AS + AV * axis:AS + AV * axis + AV], frm.rearrange("p (h c) -> p h c", h=HEADS))
                    put(scale5[r:r + 32, b:b + 1], A[vec][vfirst:vfirst + 32, :])
                put(w_n0s[:, 0:64], A["Ws_src"])
                put(w_n0s[:, 64:128], A["Ws_dst"])
                put(w_n1s[:, 0:64], A["Wl1_0"])
                put(w_n1s[:, 64:128], A["Wsc0"])
                for j in range(3):
                    r = slice(32 * j, 32 * j + 32)
                    q = slice(96 + 32 * j, 128 + 32 * j)
                    put(w_n0v[r, r], A["Wv_src"])
                    put(w_n0v[r, q], A["Wv_dst"])
                    put(w_n1v[r, r], A["Wl1_1"])
                    put(w_n1v[r, q], A["Wsc1"])
                for h in range(HEADS):
                    rows = [(40 * h, AS, A["Wps"][AS * h:AS * h + AS, :], 0)]
                    rows += [(40 * h + AS + AV * x, AV, A["Wpv"][AV * h:AV * h + AV, :], CS + CV * x) for x in range(3)]
                    for r, n, frm, c in rows:
                        cut = min(max(P - r, 0), n)
                        width = frm.shape[1]
                        if cut:
                            put(w_out_a[r:r + cut, c:c + width], frm[0:cut, :])
                        if cut < n:
                            put(w_out_b[r + cut - P:r + n - P, c:c + width], frm[cut:n, :])
                put(w_fc1[:], A["Wfc1"])
                put(w_f01[:], A["Wfc2"][:, 0:128])
                put(w_c1[0:64, 0:64], A["Wl2_s"][0:64, :])
                put(w_c1[0:64, 64:65], A["Wa"][0:64, :])
                put(w_c1[64:128, 65:97], A["Wl2_v"][0:64, :])
                for j in range(3):
                    r = slice(32 * j, 32 * j + 32)
                    put(w_f3[:, r], A["Wfc2"][:, 160:192])
                    put(w_f2[:, r], A["Wfc2"][:, 128:160])
                    put(w_c2[r, 0:64], A["Wl2_s"][64:96, :])
                    put(w_c2[r, 64:65], A["Wa"][64:96, :])
                    put(w_c3[r, r], A["Wl2_v"][64:96, :])
                sp.wait_ge(s_ext, 2)
                for k in range(2):
                    sp.dma_start(group_dram[k, :].rearrange("(c p) -> p c", p=GROUP_ROWS), ext_i[:, k, :]).then_inc(s_extw, 16)
                sp.wait_ge(s_extw, 32)
                sp.dma_start(row[:], group_dram.rearrange("k g -> (k g)").unsqueeze(0).rearrange("o (k g) -> o k g", k=2)).then_inc(s_row, 16)
                sp.dma_start(least_bc[:], group_dram[0, :].partition_broadcast(P)).then_inc(s_meta, 16)
                sp.wait_ge(s_init, 1)
                for i in range(5):
                    sp.dma_start(state[i * 10 * P:(i + 1) * 10 * P, :].rearrange("(a p) c -> p a c", p=P), init_state[:]).then_inc(s_initd, 16)
                    sp.dma_start(sums[i * 10 * P:(i + 1) * 10 * P, :].rearrange("(a p) c -> p a c", p=P), init_state[:, :, 4:4 + QW]).then_inc(s_initd, 16)
                sp.wait_ge(s_initd, 160)
                sp.wait_ge(s_meta, 16)
                sp.wait_ge(s_load, n_load[0])

            @block.gpsimd
            def _(pool):
                pool.memset(ident[:], 0.0).then_inc(s_ident, 1)
                pool.iota(iota_i[:], [[1, P]], base=0, channel_multiplier=0).then_inc(s_ident, 1)
                pool.iota(iota_ci[:], [[1, 1]], base=0, channel_multiplier=1).then_inc(s_ident, 1)
                pool.wait_ge(s_ident, 3)
                pool.affine_select(out=ident[:], in_=ident[:], compare_op=ALU.not_equal, fill=1.0, base=0,
                                   pattern=[[-1, P]], channel_multiplier=1).then_inc(s_ident, 1)
                pool.tensor_copy(iota_row[:], iota_i[:]).then_inc(s_ident, 1)
                pool.tensor_copy(iota_col[:], iota_ci[:]).then_inc(s_ident, 1)

            @block.tensor
            def _(pe):
                pe.wait_ge(s_load, n_load[0])
                nc.tensor.matmul(psum[0][0:64, 0:32], val_t[:, 0:64], wg[:], start=True, stop=True)
                nc.tensor.matmul(psum[0][0:96, 512:544], val_t[:, 64:160], wg[:], start=True, stop=True).then_inc(s_gate, 1)

            @block.vector
            def _(dve):
                for t in (w_edge, w_msg, w_val, w_n0v, w_n1v, w_out_a, w_out_b, w_c1, w_c3):
                    last = dve.memset(t[:], 0.0)
                last.then_inc(s_zero, 1)
                dve.memset(init_state[:, :, 4:SW], 0.0)
                dve.memset(init_state[:, :, 0:4], LEAST).then_inc(s_init, 1)
                for b, r, factor, *_ in value_pieces():
                    last = dve.memset(fac5[r:r + 32, b:b + 1], 0.5 * factor)
                last.then_inc(s_scale, 1)
                dve.wait_ge(s_dst, 16)
                dve.tensor_reduce(ext_i[:, 0, :], dst_g[:], axis=AX.X, op=ALU.min).then_inc(s_ext, 1)
                dve.tensor_reduce(ext_i[:, 1, :], dst_g[:], axis=AX.X, op=ALU.max).then_inc(s_ext, 1)
                dve.wait_ge(s_row, 16)
                chain = Chain(dve, s_sc, 99)
                chain.step(dve.tensor_tensor(cnt_f[:], row[:, 1, :], row[:, 0, :], ALU.subtract))
                chain.step(dve.tensor_copy(cnt_i[:], cnt_f[:]))
                chain.step(dve.tensor_scalar(cnt_i[:], cnt_i[:], 7, None, ALU.logical_shift_right))
                chain.step(dve.tensor_copy(scan_a[:], cnt_i[:]))
                chain.step(dve.tensor_scalar(scan_a[:], scan_a[:], 1.0, None, ALU.add))
                a, b, d = scan_a, scan_b, 1
                while d < NG_PAD:
                    dve.tensor_copy(b[:, 0:d], a[:, 0:d])
                    chain.step(dve.tensor_tensor(b[:, d:NG_PAD], a[:, d:NG_PAD], a[:, 0:NG_PAD - d], ALU.add))
                    a, b, d = b, a, 2 * d
                chain.step(dve.memset(window_from[:], 0))
                dve.tensor_copy(least_i[:], row[:, 0, :])
                chain.step(dve.tensor_copy(window_from[:, 1:NG_PAD + 1], a[:]))
                dve.wait_ge(s_load, n_load[0])
                dve.wait_ge(s_gate, 1)
                dve.tensor_copy(w_msg[0:64, 0, 160:192], psum[0][0:64, 0:32])
                chain.step(dve.tensor_copy(w_msg[0:96, 2, 160:192], psum[0][0:96, 512:544]))
                dve.tensor_scalar(w_msg[0:96, 2, 96:256], w_msg[0:96, 2, 96:256], R3, None, ALU.mult)
                dve.tensor_scalar(w_msg[0:96, 4, 0:96], w_msg[0:96, 4, 0:96], R2, None, ALU.mult)
                dve.tensor_scalar(w_msg[0:96, 5, 0:96], w_msg[0:96, 5, 0:96], -R2, None, ALU.mult)
                dve.tensor_scalar(w_n1s[:], w_n1s[:], 1 / math.sqrt(64.0), None, ALU.mult)
                dve.tensor_scalar(w_n1v[:], w_n1v[:], 1 / math.sqrt(32.0), None, ALU.mult)
                dve.tensor_scalar(w_c1[:], w_c1[:], 1 / 64.0, None, ALU.mult)
                dve.tensor_scalar(w_c2[:], w_c2[:], R3 / 64.0, None, ALU.mult)
                dve.tensor_scalar(w_c3[:], w_c3[:], 1 / 64.0, None, ALU.mult)
                chain.step(dve.tensor_tensor(scale5[:], scale5[:], fac5[:], ALU.mult))
                for k in range(5):
                    last = dve.tensor_scalar(w_val[:, k, :], w_val[:, k, :], scale5[:, k:k + 1], None, ALU.mult)
                chain.step(last)

    def normalize(dve, chain, x, hid, stats, s_var, s_std, turn):
        n = x.shape[2]
        big = [P, CH, n]
        chain.step(dve.tensor_reduce(stats[:, 0, :], x, axis=AX.X, op=ALU.add))
        chain.step(dve.tensor_scalar(stats[:, 0, :], stats[:, 0, :], 1.0 / n, None, ALU.mult))
        chain.step(dve.tensor_tensor(hid[0], x, stats[:, 0, :].unsqueeze(2).broadcast_to(big), ALU.subtract))
        chain.step(dve.tensor_tensor(hid[1], hid[0], hid[0], ALU.mult))
        chain.step(dve.tensor_reduce(stats[:, 1, :], hid[1], axis=AX.X, op=ALU.add))
        dve.tensor_scalar(stats[:, 1, :], stats[:, 1, :], 1.0 / n, EPS, ALU.mult, ALU.add).then_inc(s_var, 1)
        dve.wait_ge(s_std, turn)
        chain.step(dve.reciprocal(stats[:, 2, :], stats[:, 1, :]))

    def project_pe(pe, it, node, w_s, w_v, S):
        for t in range(CH):
            if t == 0:
                pe.wait_ge(S["node"], it + 1)
            nc.tensor.transpose(psum[1][0:96, t * P:(t + 1) * P], node[:, t, CS:D], ident[:])
            last = nc.tensor.transpose(psum[0][0:64, t * P:(t + 1) * P], node[:, t, 0:CS], ident[:])
        last.then_inc(S["tr"], 1)
        pe.wait_ge(S["trc"], it + 1)
        for t in range(CH):
            bank = psum[2 + t % 2]
            if t >= 2:
                pe.wait_ge(S["pjc"], it * CH + t - 1)
            nc.tensor.matmul(bank[:, 0:128], S["nts"][:, t * P:(t + 1) * P], w_s[:], start=True, stop=True)
            nc.tensor.matmul(bank[:, 512:704], S["ntv"][:, t * P:(t + 1) * P], w_v[:], start=True,
                             stop=True).then_inc(S["pj"], 1)

    def project_act(act, it, both, S):
        act.wait_ge(S["tr"], it + 1)
        nc.scalar.activation(S["nts"][:], psum[0][0:64, 0:CH * P], ACT.Copy)
        nc.scalar.activation(S["ntv"][:], psum[1][0:96, 0:CH * P], ACT.Copy).then_inc(S["trc"], 1)
        for t in range(CH):
            bank = psum[2 + t % 2]
            act.wait_ge(S["pj"], it * CH + t + 1)
            o = both[:, :, t, :]
            nc.scalar.activation(o[:, :, 0:CS], bank[:, 0:128].rearrange("p (k c) -> p k c", k=2), ACT.Copy)
            nc.scalar.activation(o[:, :, CS:D], bank[:, 512:704].rearrange("p (k c) -> p k c", k=2),
                                 ACT.Copy).then_inc(S["pjc"], 1)

    def chunk_rows(table, it):
        return table.rearrange("(c t p) f -> c p t f", t=CH, p=P)[bass.ds(it, 1), :, :, :].rearrange("c p t f -> (c p) t f")

    with ExitStack() as sx:
        def tmp(name, shape, dt=F32):
            return sx.enter_context(nc.sbuf_tensor(name, shape, dt))
        x_in = tmp("x_in", [P, CH, D])
        cen = tmp("cen", [P, CH, D])
        sq = tmp("sq", [P, CH, D])
        hn = tmp("hn", [P, CH, D])
        node = tmp("node", [P, CH, D])
        both = tmp("both", [P, 2, CH, D])
        stats = tmp("stats", [P, 3, CH])
        S = {n: sem("n0_" + n) for n in ("x", "var", "std", "node", "tr", "trc", "pj", "pjc", "ch", "tick", "out")}
        S["nts"] = tmp("nts", [64, CH * P])
        S["ntv"] = tmp("ntv", [96, CH * P])

        with nc.Block() as block:
            @block.sync
            def _(sp):
                with sp.Fori(0, NCH) as it:
                    sp.dma_start(x_in[:], chunk_rows(A["x"], it)).then_inc(S["x"], 16)
                    sp.wait_ge(S["pjc"], it * CH + CH)
                    for k, table in enumerate((src_tab, dst_tab)):
                        sp.dma_start(chunk_rows(table, it), both[:, k, :, :]).then_inc(S["out"], 16)
                    wait_apart(sp, S["out"], it * 32 + 32, S["tick"])

            @block.vector
            def _(dve):
                chain = Chain(dve, S["ch"], 22)
                with dve.Fori(0, NCH) as it:
                    chain.begin(it)
                    dve.wait_ge(S["x"], it * 16 + 16)
                    normalize(dve, chain, x_in[:], (cen[:], sq[:]), stats, S["var"], S["std"], it * 3 + 1)
                    chain.step(dve.tensor_tensor(cen[:], cen[:], stats[:, 2, :].unsqueeze(2).broadcast_to([P, CH, D]), ALU.mult))
                    chain.step(dve.tensor_scalar(hn[:], cen[:], 0.0, None, ALU.max))
                    chain.step(dve.tensor_tensor(keep[:, bass.ds(it * CH, CH), :], x_in[:], hn[:], ALU.add))
                    s, v = hn[:, :, 0:CS], hn[:, :, CS:D]
                    normalize(dve, chain, s, (cen[:, :, 0:CS], sq[:, :, 0:CS]), stats, S["var"], S["std"], it * 3 + 2)
                    small = [P, CH, CS]
                    chain.step(dve.tensor_tensor(cen[:, :, 0:CS], cen[:, :, 0:CS], stats[:, 2, :].unsqueeze(2).broadcast_to(small), ALU.mult))
                    chain.step(dve.tensor_tensor(cen[:, :, 0:CS], cen[:, :, 0:CS], gam_s[:].unsqueeze(1).broadcast_to(small), ALU.mult))
                    chain.step(dve.tensor_tensor(node[:, :, 0:CS], cen[:, :, 0:CS], bet_s[:].unsqueeze(1).broadcast_to(small), ALU.add))
                    chain.step(dve.tensor_tensor(sq[:, :, CS:D], v, v, ALU.mult))
                    chain.step(dve.tensor_reduce(stats[:, 1, :], sq[:, :, CS:D], axis=AX.X, op=ALU.add))
                    dve.tensor_scalar(stats[:, 1, :], stats[:, 1, :], 1.0 / CV, EPS, ALU.mult, ALU.add).then_inc(S["var"], 1)
                    dve.wait_ge(S["std"], it * 3 + 3)
                    chain.step(dve.reciprocal(stats[:, 2, :], stats[:, 1, :]))
                    chain.step(dve.tensor_tensor(cen[:, :, CS:D], v, stats[:, 2, :].unsqueeze(2).broadcast_to([P, CH, 3 * CV]), ALU.mult))
                    for x in range(3):
                        last = dve.tensor_tensor(node[:, :, CS + CV * x:CS + CV * x + CV], cen[:, :, CS + x:D:3],
                                                 gam_v[:].unsqueeze(1).broadcast_to([P, CH, CV]), ALU.mult)
                    last.then_inc(S["node"], 1)
                    chain.end()
            @block.scalar
            def _(act):
                with act.Fori(0, NCH) as it:
                    for k in range(3):
                        act.wait_ge(S["var"], it * 3 + k + 1)
                        nc.scalar.activation(stats[:, 1, :], stats[:, 1, :], ACT.Sqrt).then_inc(S["std"], 1)
                    project_act(act, it, both, S)

            @block.tensor
            def _(pe):
                with pe.Fori(0, NCH) as it:
                    project_pe(pe, it, node, w_n0s, w_n0v, S)


    layer0(nc, ctx, A, locals())
    node1(nc, ctx, A, locals())
    layer1(nc, ctx, A, locals())
    node2(nc, ctx, A, locals(), out)


def value_pieces():
    out = []
    for k in range(4):
        for j in range(3):
            r = 32 * j
            if k == 0:
                out.append((0, r, 1.0, "Wv_vlin", 64, j, "w2_vs", 0))
            elif j == k - 1:
                out.append((k, r, R3, "Ws_vlin", 64, None, "w2_vv0", 0))
            elif k - 1 == (j + 1) % 3:
                out.append((k, r, R2, "Wv_vlin", 96, (j + 2) % 3, "w2_vv1", 0))
            else:
                out.append((k, r, -R2, "Wv_vlin", 96, (j + 1) % 3, "w2_vv1", 0))
        for b, r, first in ((k, 96, 0), (4, 32 * k, 32)):
            if k == 0:
                out.append((b, r, 1.0, "Ws_vlin", first, None, "w2_ss", first))
            else:
                out.append((b, r, 1.0, "Wv_vlin", first, k - 1, "w2_sv", first))
    return out


def window_numbers(eng, window_from, g):
    first = eng.value_load(window_from[0:1, bass.ds(g, 1)], min_val=0, max_val=MAX_W)
    end = eng.value_load(window_from[0:1, bass.ds(g + 1, 1)], min_val=0, max_val=MAX_W)
    return first, end


def schedule(step):
    def both(eng):
        step(0, 0, 0, True, False)
        with eng.Fori(0, NG // 2) as i:
            step(i * 2 + 1, 1, i, True, True)
            step(i * 2 + 2, 0, i + 1, True, True)
        step(NG, NG % 2, NG // 2, False, True)
    return both


def previous(slot, use):
    return 1 - slot, use if slot == 1 else use - 1


def group_of(ap, g):
    return ap[g] if isinstance(g, int) else ap[bass.ds(g, 1)].squeeze(0)

def layer0(nc, ctx, A, K):
    (ident, iota_row, iota_col, least_bc, window_from, idx_all, w_edge, w_msg, w_val, adot, psum, state,
     src_tab, dst_tab) = (K[n] for n in (
        "ident", "iota_row", "iota_col", "least_bc", "window_from", "idx_all", "w_edge", "w_msg", "w_val",
        "adot", "psum", "state", "src_tab", "dst_tab"))
    s = {n: ctx.enter_context(nc.semaphore("l0_" + n)) for n in (
        "edge0", "edge1", "wide0", "wide1", "got0", "got1", "summed", "scaled", "turned", "turned_copied",
        "logit_turned", "logit_copied", "value_turned", "weighted", "block_done", "message", "tanh", "relu",
        "gated", "gate", "logit", "logit_step", "value_block", "value", "masks", "mask_step", "top", "top_at_edge",
        "shifted", "expd", "value_scaled", "rescale", "factors", "window_sum", "merged", "win_step",
        "state_in", "state_out", "tick", "tick_v", "left", "indexed", "rel", "at_node", "scalars", "tick_s")}
    with ExitStack() as sx:
        def tmp(name, shape, dt=F32):
            return sx.enter_context(nc.sbuf_tensor(name, shape, dt))
        idx = [tmp(f"idx{i}", [P, 2 * TILES], I32) for i in range(2)]
        got_src = [tmp(f"got_src{i}", [P, TILES, D]) for i in range(2)]
        got_dst = [tmp(f"got_dst{i}", [P, TILES, D]) for i in range(2)]
        msg = [tmp(f"msg{i}", [P, TILES, CS + D]) for i in range(2)]
        rbf4 = [tmp(f"rbf4{i}", [64, GE]) for i in range(2)]
        y16 = [tmp(f"y16{i}", [64, GE]) for i in range(2)]
        edge = [tmp(f"edge{i}", [64, GE]) for i in range(2)]
        y_all = [tmp(f"y_all{i}", [P, 4, GE]) for i in range(2)]
        y_quad = [tmp(f"y_quad{i}", [P, GE]) for i in range(2)]
        dst_bc = [tmp(f"dst_bc{i}", [P, GE], I32) for i in range(2)]
        sT2 = tmp("sT2", [P, GE])
        vT = tmp("vT", [96, GE])
        blocks = tmp("blocks", [P, 6, GE])
        th = tmp("th", [P, TILES, 96])
        rl = tmp("rl", [P, TILES, 64])
        lg = tmp("lg", [P, TILES, 64])
        gated = [tmp(f"gated{i}", [P, TILES, 256]) for i in range(2)]
        gates = tmp("gates", [P, TILES, CV])
        logits = [tmp(f"logits{i}", [P, TILES * HEADS]) for i in range(2)]
        logit_bc = tmp("logit_bc", [P, HEADS, GE])
        vblocks = tmp("vblocks", [P, 5, GE])
        far = tmp("far", [P, GE])
        at_node = tmp("at_node", [P, GE])
        to_node = tmp("to_node", [P, TILES, P])
        dst_f = tmp("dst_f", [P, TILES])
        rel = tmp("rel", [P, TILES])
        first_node = tmp("first_node", [P, 1])
        junk = tmp("junk", [P, HEADS, GE])
        top = tmp("top", [P, HEADS])
        shift = tmp("shift", [P, TILES * HEADS])
        vals = tmp("vals", [P, TILES * HEADS, HW])
        st_in = tmp("st_in", [P, SW])
        st_out = tmp("st_out", [P, SW])
        diff = tmp("diff", [P, 2 * HEADS])
        fac = tmp("fac", [P, 2 * HEADS])
        part = tmp("part", [P, 2, HEADS, HW])

        pT, pW, pM, pV = psum
        messages = pM[:].rearrange("p (t c) -> p t c", t=TILES)
        def value_tile(t):
            o = 512 * (t // 2) + D * (t % 2)
            return pV[:, o:o + D]
        win = pV[:, 320:320 + HEADS * HW]
        top_edge = pV[:, 512 + 320:512 + 320 + TILES * HEADS]
        ebank = lambda b: pW[:, 512 * (b % 2):512 * (b % 2) + 512]

        with nc.Block() as block:
            @block.sync
            def _(sp):
                def load_edge(g, slot):
                    for k in range(4):
                        rows = slice(NB * k, NB * k + NB)
                        sp.dma_start(rbf4[slot][rows, :], group_of(A["rbf"], g)).then_inc(s[f"edge{slot}"], 16)
                        sp.dma_start(y16[slot][rows, :], group_of(A["y"], g)[k, :].partition_broadcast(NB)).then_inc(s[f"edge{slot}"], 16)

                def step(g, slot, use, now, before):
                    if now:
                        if not before:
                            load_edge(0, 0)
                        else:
                            wait_apart(sp, s["scaled"], g, s["tick_s"])
                        load_edge(g + 1, 1 - slot)
                        if before:
                            wait_apart(sp, s["left"], g, s["tick_s"])
                        y = group_of(A["y"], g)
                        sp.dma_start(y_all[slot][:], y.partition_broadcast(P)).then_inc(s[f"wide{slot}"], 16)
                        for k in range(4):
                            sp.dma_start(y_quad[slot][32 * k:32 * k + 32, :], y[k, :].partition_broadcast(32)).then_inc(s[f"wide{slot}"], 16)
                        sp.dma_start(dst_bc[slot][:], group_of(A["dst_rows"], g).partition_broadcast(P)).then_inc(s[f"wide{slot}"], 16)
                    if before:
                        window_rows(nc, sp, g - 1, window_from, K["least_i"], state, st_in, st_out, s)

                sp.sem_inc(s["state_out"], 16)
                schedule(step)(sp)
                total = sp.value_load(window_from[0:1, NG:NG + 1], min_val=1, max_val=MAX_W)
                wait_apart(sp, s["state_out"], total * 16 + 16, s["tick_s"])

            @block.gpsimd
            def _(pool):
                def wait(sm, value):
                    wait_apart(pool, sm, value, s["tick"])

                def gather(g, slot, use, fresh):
                    if not fresh:
                        wait(s[f"got{slot}"], use * 128)
                    pool.tensor_copy(idx[slot][:], idx_all[:, bass.ds(g, 1), :].rearrange("p a c -> p (a c)")).then_inc(s["indexed"], 1)
                    wait(s["indexed"], g + 1)
                    if not fresh:
                        wait(s["summed"], g - 1)
                    for t in range(TILES):
                        for buf, table, c in ((got_src, src_tab, t), (got_dst, dst_tab, TILES + t)):
                            pool.indirect_dma_start(
                                out=buf[slot][:, t, :], out_offset=None, in_=table[:, :],
                                in_offset=bass.IndirectOffsetOnAxis(ap=idx[slot][:, c:c + 1], axis=0)
                            ).then_inc(s[f"got{slot}"], 16)

                def combine(g, slot, use, fresh):
                    wait(s[f"got{slot}"], use * 128 + 128)
                    if not fresh:
                        wait(s["turned"], g - 1)
                    twice = [P, TILES, 2, CS]
                    pool.tensor_tensor(msg[slot][:, :, 0:2 * CS].rearrange("p t (k c) -> p t k c", k=2),
                                       got_src[slot][:, :, 0:CS].unsqueeze(2).broadcast_to(twice),
                                       got_dst[slot][:, :, 0:CS].unsqueeze(2).broadcast_to(twice), ALU.add)
                    pool.tensor_tensor(msg[slot][:, :, 2 * CS:], got_src[slot][:, :, CS:D], got_dst[slot][:, :, CS:D],
                                       ALU.add).then_inc(s["summed"], 1)
                    wait(s[f"edge{slot}"], use * 128 + 128)
                    if not fresh:
                        wait(s["weighted"], g * 6 - 6)
                    pool.tensor_tensor(edge[slot][:], rbf4[slot][:], y16[slot][:], ALU.mult).then_inc(s["scaled"], 1)

                def leave(g, slot, use, more):
                    wait(s[f"wide{slot}"], use * 96 + 96)
                    window_masks(pool, wait, g, K, s, dst_bc[slot], dst_f, rel, first_node, to_node, far, at_node)
                    if more:
                        gather(g + 2, slot, use + 1, False)
                        combine(g + 2, slot, use + 1, False)

                pool.sem_inc(s["window_sum"], 1)
                for g in range(2):
                    gather(g, g, 0, True)
                    combine(g, g, 0, True)
                with pool.Fori(0, NG // 2) as i:
                    leave(i * 2, 0, i, True)
                    leave(i * 2 + 1, 1, i, True)
                leave(NG - 1, 0, NG // 2, False)

            @block.tensor
            def _(pe):
                def step(g, slot, use, now, before):
                    if now:
                        pe.wait_ge(s["summed"], g + 1)
                        for t in range(TILES):
                            c = slice(P * t, P * t + P)
                            nc.tensor.transpose(pT[:, c], msg[slot][:, t, 0:2 * CS], ident[:])
                            last = nc.tensor.transpose(pT[0:96, 512 + P * t:640 + P * t], msg[slot][:, t, 2 * CS:], ident[:])
                        last.then_inc(s["turned"], 1)
                    if before:
                        old, _ = previous(slot, use)
                        pe.wait_ge(s["logit"], g)
                        for h in range(HEADS):
                            if h >= 2:
                                pe.wait_ge(s["logit_copied"], g * 4 - 4 + h - 1)
                            for t in range(TILES):
                                c = t * HEADS + h
                                last = nc.tensor.transpose(ebank(h)[:, P * t:P * t + P],
                                                           logits[old][:, c:c + 1].broadcast_to([P, P]), ident[:])
                            last.then_inc(s["logit_turned"], 1)
                        pe.wait_ge(s["gated"], g)
                        pe.wait_ge(s["scalars"], g)
                        if now:
                            pe.wait_ge(s["turned_copied"], g + 1)
                        for t in range(TILES):
                            nc.tensor.transpose(pT[:, P * t:P * t + P], gated[old][:, t, 0:P], ident[:])
                            last = nc.tensor.transpose(pT[:, 512 + P * t:640 + P * t],
                                                       gated[old][:, t, P:2 * P], ident[:])
                        last.then_inc(s["value_turned"], 1)
                    if now:
                        for b in range(6):
                            m = P if b < 2 else 96
                            if b == 0:
                                pe.wait_ge(s["scaled"], g + 1)
                            if b < 2 and before:
                                pe.wait_ge(s["logit_copied"], g * 4 - 1 + b)
                            if b >= 2:
                                pe.wait_ge(s["block_done"], g * 6 + b - 1)
                            nc.tensor.matmul(ebank(b)[0:m, :], w_edge[:, b, 0:m], edge[slot][:], start=True,
                                             stop=True).then_inc(s["weighted"], 1)
                        pe.wait_ge(s["block_done"], g * 6 + 6)
                        for t in range(TILES):
                            for b, c0, c1 in ((0, 0, 256), (1, 32, 96), (2, 96, 256), (3, 0, 96), (4, 0, 96), (5, 0, 96)):
                                m = P if b < 2 else 96
                                last = nc.tensor.matmul(messages[:, t, c0:c1], blocks[0:m, b, P * t:P * t + P],
                                                        w_msg[0:m, b, c0:c1], start=b == 0, stop=b == 5)
                        last.then_inc(s["message"], 1)
                    if before:
                        pe.wait_ge(s["value_block"], g * 5)
                        for t in range(TILES):
                            for b in range(5):
                                last = nc.tensor.matmul(value_tile(t), vblocks[:, b, P * t:P * t + P], w_val[:, b, :],
                                                        start=b == 0, stop=b == 4)
                        last.then_inc(s["value"], 1)
                        w0, w1 = window_numbers(pe, window_from, g - 1)
                        with pe.Fori(w0, w1) as w:
                            pe.wait_ge(s["masks"], w + 1)
                            pe.wait_ge(s["top"], w + 1)
                            for t in range(TILES):
                                last = nc.tensor.matmul(top_edge[:, HEADS * t:HEADS * t + HEADS], at_node[:, P * t:P * t + P],
                                                        top[:], start=True, stop=True)
                            last.then_inc(s["top_at_edge"], 1)
                            pe.wait_ge(s["merged"], w + 1)
                            pe.wait_ge(s["value_scaled"], w + 1)
                            for t in range(TILES):
                                last = nc.tensor.matmul(win, to_node[:, t, :],
                                                        vals[:, HEADS * t:HEADS * t + HEADS, :].rearrange("p h c -> p (h c)"),
                                                        start=t == 0, stop=t == TILES - 1)
                            last.then_inc(s["window_sum"], 1)
                schedule(step)(pe)

            @block.scalar
            def _(act):
                def step(g, slot, use, now, before):
                    if now:
                        act.wait_ge(s["turned"], g + 1)
                        if before:
                            act.wait_ge(s["block_done"], g * 6)
                        nc.scalar.activation(sT2[:], pT[:, 0:512], ACT.Copy)
                        nc.scalar.activation(vT[:], pT[0:96, 512:1024], ACT.Copy).then_inc(s["turned_copied"], 1)
                    if before:
                        act.wait_ge(s["left"], g)
                        for h in range(HEADS):
                            act.wait_ge(s["logit_turned"], g * 4 - 4 + h + 1)
                            nc.scalar.activation(logit_bc[:, h, :], ebank(h), ACT.Copy).then_inc(s["logit_copied"], 1)
                    if now:
                        act.wait_ge(s["message"], g + 1)
                        nc.scalar.activation(th[:], messages[:, :, 96:192], ACT.Tanh, scale=0.5).then_inc(s["tanh"], 1)
                        nc.scalar.activation(rl[:], messages[:, :, 192:256], ACT.Relu, scale=0.8).then_inc(s["relu"], 1)
                        act.wait_ge(s["tanh"], g + 1)
                        nc.scalar.activation(gated[slot][:, :, 96:128], th[:, :, 0:32], ACT.Copy, bias=1.0)
                        nc.scalar.activation(gated[slot][:, :, 128:256].rearrange("p t (k c) -> p t k c", k=4),
                                             th[:, :, 32:64].unsqueeze(2).broadcast_to([P, TILES, 4, 32]),
                                             ACT.Copy, bias=1.0).then_inc(s["scalars"], 1)
                    if before:
                        w0, w1 = window_numbers(act, window_from, g - 1)
                        with act.Fori(w0, w1) as w:
                            act.wait_ge(s["window_sum"], w + 1)
                            act.wait_ge(s["shifted"], w + 1)
                            nc.scalar.activation(vals[:, :, 0], shift[:], ACT.Exp).then_inc(s["expd"], 1)
                            act.wait_ge(s["rescale"], w + 1)
                            nc.scalar.activation(fac[:], diff[:], ACT.Exp).then_inc(s["factors"], 1)
                schedule(step)(act)

            @block.vector
            def _(dve):
                def step(g, slot, use, now, before):
                    if now:
                        for b in range(6):
                            m = P if b < 2 else 96
                            dve.wait_ge(s["weighted"], g * 6 + b + 1)
                            if b == 0:
                                dve.wait_ge(s["turned_copied"], g + 1)
                            dve.tensor_tensor(blocks[0:m, b, :], ebank(b)[0:m, :], (sT2 if b < 2 else vT)[0:m, :],
                                              ALU.mult).then_inc(s["block_done"], 1)
                    if before:
                        old, old_use = previous(slot, use)
                        dve.wait_ge(s[f"wide{old}"], old_use * 96 + 96)
                        dve.wait_ge(s["value_turned"], g)
                        for k in range(4):
                            dve.tensor_tensor(vblocks[:, k, :], pT[:, 0:512], y_all[old][:, k, :], ALU.mult).then_inc(s["value_block"], 1)
                        dve.tensor_tensor(vblocks[:, 4, :], pT[:, 512:1024], y_quad[old][:], ALU.mult).then_inc(s["value_block"], 1)
                    if now:
                        dve.wait_ge(s["tanh"], g + 1)
                        dve.tensor_scalar(gates[:], th[:, :, 64:96], 1.0, None, ALU.add).then_inc(s["gate"], 1)
                        dve.wait_ge(s["gate"], g + 1)
                        dve.wait_ge(s["relu"], g + 1)
                        dve.tensor_tensor(gated[slot][:, :, 0:96].rearrange("p t (x d) -> p t x d", x=3),
                                          messages[:, :, 0:96].rearrange("p t (x d) -> p t x d", x=3),
                                          gates[:].unsqueeze(2).broadcast_to([P, TILES, 3, CV]),
                                          ALU.mult).then_inc(s["gated"], 1)
                        dve.scalar_tensor_tensor(lg[:], messages[:, :, 192:256], 0.2, rl[:], ALU.mult, ALU.add).then_inc(s["logit_step"], 1)
                        dve.wait_ge(s["logit_step"], g * 2 + 1)
                        dve.tensor_tensor(lg[:], lg[:], adot[:].unsqueeze(1).broadcast_to([P, TILES, 64]), ALU.mult).then_inc(s["logit_step"], 1)
                        dve.wait_ge(s["logit_step"], g * 2 + 2)
                        dve.tensor_reduce(logits[slot][:], lg[:].rearrange("p t (h c) -> p (t h) c", h=HEADS), axis=AX.X,
                                          op=ALU.add).then_inc(s["logit"], 1)
                    if before:
                        w0, w1 = window_numbers(dve, window_from, g - 1)
                        dve.wait_ge(s["logit_copied"], g * 4)
                        dve.sem_inc(s["tick_v"], 1)
                        with dve.Fori(w0, w1) as w:
                            dve.wait_ge(s["masks"], w + 1)
                            dve.sem_inc(s["tick_v"], 1)
                            for h in range(HEADS):
                                last = dve.tensor_tensor_reduce(out=junk[:, h, :], in0=logit_bc[:, h, :], in1=far[:], scale=1.0,
                                                                scalar=LEAST, op0=ALU.add, op1=ALU.max, accum_out=top[:, h:h + 1])
                            last.then_inc(s["top"], 1)
                            dve.wait_ge(s["top_at_edge"], w + 1)
                            dve.tensor_tensor(shift[:], logits[old][:], top_edge, ALU.subtract).then_inc(s["win_step"], 1)
                            dve.wait_ge(s["win_step"], w * 3 + 1)
                            dve.tensor_scalar(shift[:], shift[:], 1.0, None, ALU.min).then_inc(s["shifted"], 1)
                            dve.wait_ge(s["state_in"], w * 16 + 16)
                            dve.tensor_tensor(st_out[:, 0:HEADS], st_in[:, 0:HEADS], top[:], ALU.max).then_inc(s["win_step"], 1)
                            dve.wait_ge(s["win_step"], w * 3 + 2)
                            dve.tensor_tensor(diff[:, 0:HEADS], st_in[:, 0:HEADS], st_out[:, 0:HEADS], ALU.subtract)
                            dve.tensor_tensor(diff[:, HEADS:2 * HEADS], top[:], st_out[:, 0:HEADS], ALU.subtract).then_inc(s["rescale"], 1)
                            dve.wait_ge(s["value"], g)
                            dve.wait_ge(s["expd"], w + 1)
                            dve.tensor_tensor(vals[:, :, 1:HW].rearrange("p (b h) c -> p b h c", b=2),
                                              pV[:].rearrange("p (b c) -> p b c", b=2)[:, :, 0:320].rearrange("p b (h c) -> p b h c", c=HW - 1),
                                              vals[:, :, 0:1].rearrange("p (b h) c -> p b h c", b=2).broadcast_to([P, 2, 2 * HEADS, HW - 1]),
                                              ALU.mult).then_inc(s["value_scaled"], 1)
                            dve.wait_ge(s["factors"], w + 1)
                            dve.tensor_tensor(part[:, 0, :, :], st_in[:, HEADS:SW].rearrange("p (h c) -> p h c", h=HEADS),
                                              fac[:, 0:HEADS].unsqueeze(2).broadcast_to([P, HEADS, HW]), ALU.mult)
                            dve.wait_ge(s["window_sum"], w + 2)
                            dve.tensor_tensor(part[:, 1, :, :], win.rearrange("p (h c) -> p h c", h=HEADS),
                                              fac[:, HEADS:2 * HEADS].unsqueeze(2).broadcast_to([P, HEADS, HW]), ALU.mult).then_inc(s["win_step"], 1)
                            dve.wait_ge(s["win_step"], w * 3 + 3)
                            dve.tensor_tensor(st_out[:, HEADS:SW].rearrange("p (h c) -> p h c", h=HEADS), part[:, 0, :, :],
                                              part[:, 1, :, :], ALU.add).then_inc(s["merged"], 1)
                        dve.wait_ge(s["merged"], w1 + 1)
                        dve.sem_inc(s["left"], 1)
                dve.sem_inc(s["merged"], 1)
                dve.sem_inc(s["left"], 1)
                schedule(step)(dve)


def window_rows(nc, sp, g, window_from, least_i, table, st_in, st_out, s):
    w0, w1 = window_numbers(sp, window_from, g)
    first_row = sp.value_load(least_i[0:1, bass.ds(g, 1)], min_val=0, max_val=N_NODES)
    with sp.Fori(w0, w1) as w:
        row = nc.s_assert_within(first_row + (w - w0) * P, 0, STATE_ROWS - P)
        wait_apart(sp, s["state_out"], w * 16 + 16, s["tick_s"])
        sp.dma_start(st_in[:], table[bass.ds(row, P), :]).then_inc(s["state_in"], 16)
        wait_apart(sp, s["merged"], w + 2, s["tick_s"])
        sp.dma_start(table[bass.ds(row, P), :], st_out[:]).then_inc(s["state_out"], 16)


def window_masks(pool, wait, g, K, s, dst_bc, dst_f, rel, first_node, to_node, far=None, at_node=None):
    w0, w1 = window_numbers(pool, K["window_from"], g)
    least = K["least_bc"][:, bass.ds(g, 1)]
    pool.tensor_copy(dst_f[:], K["idx_all"][:, bass.ds(g, 1), TILES:2 * TILES].rearrange("p a c -> p (a c)")).then_inc(s["mask_step"], 1)
    wait(s["mask_step"], g + 1)
    pool.tensor_tensor(rel[:], dst_f[:], least.broadcast_to([P, TILES]), ALU.subtract)
    pool.tensor_tensor(first_node[:], K["iota_col"][:], least, ALU.add).then_inc(s["rel"], 1)
    with pool.Fori(w0, w1) as w:
        wait(s["window_sum"], w + 1)
        wait(s["rel"], w + g + 1)
        if far is not None:
            pool.tensor_scalar(at_node[:], dst_bc[:], first_node[:, 0:1], None, ALU.is_equal).then_inc(s["at_node"], 1)
        for t in range(TILES):
            last = pool.tensor_scalar(to_node[:, t, :], K["iota_row"][:], rel[:, t:t + 1], None, ALU.is_equal)
        if far is not None:
            wait(s["at_node"], w + 1)
            last = pool.tensor_scalar(far[:], at_node[:], 1.0, -LEAST, ALU.subtract, ALU.mult)
        last.then_inc(s["masks"], 1)
        wait(s["masks"], w + 1)
        pool.tensor_scalar(rel[:], rel[:], float(-P), None, ALU.add)
        pool.tensor_scalar(first_node[:], first_node[:], float(P), None, ALU.add).then_inc(s["rel"], 1)


def node1(nc, ctx, A, K):
    keep, ident, psum, state, attr = (K[n] for n in ("keep", "ident", "psum", "state", "attr"))
    chunk_rows, normalize, project_pe, project_act = (K[n] for n in ("chunk_rows", "normalize", "project_pe", "project_act"))
    with ExitStack() as sx:
        def tmp(name, shape, dt=F32):
            return sx.enter_context(nc.sbuf_tensor(name, shape, dt))
        st = tmp("st", [P, CH, SW])
        agg = tmp("agg", [P, CH, D])
        den = tmp("den", [P, 2, CH, HEADS])
        agg_ta = tmp("agg_ta", [P, CH * P])
        agg_tb = tmp("agg_tb", [CV, CH * P])
        res = tmp("res", [P, CH, D])
        x1 = tmp("x1", [P, CH, D])
        cen = tmp("cen1", [P, CH, D])
        sq = tmp("sq1", [P, CH, D])
        node = tmp("node1", [P, CH, D])
        both = tmp("both1", [P, 2, CH, D])
        f_out = tmp("f_out", [P, CH, D])
        stats = tmp("stats1", [P, 3, CH])
        S = {n: ctx.enter_context(nc.semaphore("n1_" + n)) for n in (
            "x", "var", "std", "node", "tr", "trc", "pj", "pjc", "ch", "tick", "out", "agg", "at", "atc", "res", "resc", "f")}
        S["nts"] = tmp("nts1", [64, CH * P])
        S["ntv"] = tmp("ntv1", [96, CH * P])

        with nc.Block() as block:
            @block.sync
            def _(sp):
                with sp.Fori(0, NCH) as it:
                    sp.dma_start(st[:], chunk_rows(state[0:NODES_PAD, :], it)).then_inc(S["x"], 16)
                    sp.wait_ge(S["f"], it + 1)
                    sp.dma_start(chunk_rows(K["f_tab"], it), f_out[:]).then_inc(S["out"], 16)
                    wait_apart(sp, S["out"], it * 16 + 16, S["tick"])

            @block.vector
            def _(dve):
                chain = Chain(dve, S["ch"], 14)
                with dve.Fori(0, NCH) as it:
                    chain.begin(it)
                    mine = bass.ds(it * CH, CH)
                    dve.wait_ge(S["x"], it * 16 + 16)
                    by_head = st[:, :, HEADS:SW].rearrange("p t (h c) -> p t h c", h=HEADS)
                    chain.step(dve.tensor_scalar(den[:, 0, :, :], by_head[:, :, :, 0], 1e-16, None, ALU.add))
                    chain.step(dve.reciprocal(den[:, 1, :, :], den[:, 0, :, :]))
                    dve.tensor_tensor(agg[:].rearrange("p t (h c) -> p t h c", h=HEADS), by_head[:, :, :, 1:HW],
                                      den[:, 1, :, :].unsqueeze(3).broadcast_to([P, CH, HEADS, HW - 1]), ALU.mult).then_inc(S["agg"], 1)
                    dve.wait_ge(S["resc"], it * CH + CH)
                    chain.step(dve.tensor_tensor(x1[:, :, 0:CS], res[:, :, 0:CS], keep[:, mine, 0:CS], ALU.add))
                    for x in range(3):
                        last = dve.tensor_tensor(x1[:, :, CS + x:D:3], res[:, :, CS + CV * x:CS + CV * x + CV],
                                                 keep[:, mine, CS + x:D:3], ALU.add)
                    chain.step(last)
                    normalize(dve, chain, x1[:], (cen[:], sq[:]), stats, S["var"], S["std"], it + 1)
                    chain.step(dve.tensor_tensor(cen[:], cen[:], stats[:, 2, :].unsqueeze(2).broadcast_to([P, CH, D]), ALU.mult))
                    dve.tensor_scalar(node[:, :, 0:CS], cen[:, :, 0:CS], 0.0, None, ALU.max)
                    for x in range(3):
                        last = dve.tensor_scalar(node[:, :, CS + CV * x:CS + CV * x + CV], cen[:, :, CS + x:D:3], 0.0, None, ALU.max)
                    last.then_inc(S["node"], 1)
                    dve.wait_ge(S["pjc"], it * CH + CH)
                    by_attr = attr[:, mine].unsqueeze(2).broadcast_to([P, CH, D])
                    dve.tensor_tensor(f_out[:], both[:, 0, :, :], by_attr, ALU.mult).then_inc(S["f"], 1)
                    chain.step(dve.tensor_tensor(res[:], both[:, 1, :, :], by_attr, ALU.mult))
                    chain.step(dve.tensor_tensor(keep[:, mine, 0:CS], res[:, :, 0:CS], x1[:, :, 0:CS], ALU.add))
                    for x in range(3):
                        last = dve.tensor_tensor(keep[:, mine, CS + x:D:3], res[:, :, CS + CV * x:CS + CV * x + CV],
                                                 x1[:, :, CS + x:D:3], ALU.add)
                    chain.step(last)
                    chain.end()

            @block.scalar
            def _(act):
                with act.Fori(0, NCH) as it:
                    act.wait_ge(S["at"], it + 1)
                    nc.scalar.activation(agg_ta[:], psum[0][:, 0:CH * P], ACT.Copy)
                    nc.scalar.activation(agg_tb[:], psum[1][0:CV, 0:CH * P], ACT.Copy).then_inc(S["atc"], 1)
                    for t in range(CH):
                        act.wait_ge(S["res"], it * CH + t + 1)
                        nc.scalar.activation(res[:, t, :], psum[2 + t % 2][:, 0:D], ACT.Copy).then_inc(S["resc"], 1)
                    act.wait_ge(S["var"], it + 1)
                    nc.scalar.activation(stats[:, 1, :], stats[:, 1, :], ACT.Sqrt).then_inc(S["std"], 1)
                    project_act(act, it, both, S)

            @block.tensor
            def _(pe):
                with pe.Fori(0, NCH) as it:
                    pe.wait_ge(S["agg"], it + 1)
                    for t in range(CH):
                        c = slice(t * P, (t + 1) * P)
                        nc.tensor.transpose(psum[0][:, c], agg[:, t, 0:P], ident[:])
                        last = nc.tensor.transpose(psum[1][0:CV, c], agg[:, t, P:D], ident[:])
                    last.then_inc(S["at"], 1)
                    pe.wait_ge(S["atc"], it + 1)
                    for t in range(CH):
                        c = slice(t * P, (t + 1) * P)
                        if t >= 2:
                            pe.wait_ge(S["resc"], it * CH + t - 1)
                        nc.tensor.matmul(psum[2 + t % 2][:, 0:D], agg_ta[:, c], K["w_out_a"][:], start=True, stop=False)
                        nc.tensor.matmul(psum[2 + t % 2][:, 0:D], agg_tb[:, c], K["w_out_b"][:], start=False,
                                         stop=True).then_inc(S["res"], 1)
                    project_pe(pe, it, node, K["w_n1s"], K["w_n1v"], S)


def layer1(nc, ctx, A, K):
    ident, idx_all, window_from, psum, sums, f_tab = (K[n] for n in ("ident", "idx_all", "window_from", "psum", "sums", "f_tab"))
    s = {n: ctx.enter_context(nc.semaphore("l1_" + n)) for n in (
        "edge0", "edge1", "got0", "got1", "indexed", "doubled", "hidden_raw", "hid_tanh", "hidden", "turned",
        "turned_copied", "weight", "product", "scaled_product", "edge_sums", "scal_copied", "vec_step", "edge_value", "masks", "mask_step", "rel",
        "window_sum", "merged", "state_in", "state_out", "tick", "tick_s", "ones")}
    with ExitStack() as sx:
        def tmp(name, shape, dt=F32):
            return sx.enter_context(nc.sbuf_tensor(name, shape, dt))
        idx = [tmp(f"idx1{i}", [P, TILES], I32) for i in range(2)]
        got = [tmp(f"gotf{i}", [P, TILES, D]) for i in range(2)]
        got2 = [tmp(f"gotd{i}", [P, TILES, 2 * CS]) for i in range(2)]
        rbf = [tmp(f"rbf{i}", [NB, GE]) for i in range(2)]
        y_scal = [tmp(f"y_scal{i}", [P, GE]) for i in range(2)]
        y_vec = [tmp(f"y_vec{i}", [96, GE]) for i in range(2)]
        y_edge = [tmp(f"y_edge{i}", [P, TILES, 4]) for i in range(2)]
        th = tmp("th1", [64, GE])
        hid = tmp("hid", [64, GE])
        e0T = tmp("e0T", [P, GE])
        e1T = tmp("e1T", [96, GE])
        prod = tmp("prod", [P, 3, GE])
        val = [tmp(f"val{i}", [P, TILES, QW]) for i in range(2)]
        vec = tmp("vec", [P, 2, TILES, 96])
        to_node = tmp("to_node1", [P, TILES, P])
        dst_f = tmp("dst_f1", [P, TILES])
        rel = tmp("rel1", [P, TILES])
        first_node = tmp("first_node1", [P, 1])
        st_in = tmp("st_in1", [P, QW])
        st_out = tmp("st_out1", [P, QW])
        pT, pW, pE, pS = psum
        win = pS[:, 0:QW]
        loads = 16 * 6

        def edge_tile(t, c0, c1):
            o = 512 * (t // 2) + 193 * (t % 2)
            return pE[:, o + c0:o + c1]

        by_tile = pE[:].rearrange("p (b c) -> p b c", b=2)[:, :, 0:386].rearrange("p b (t c) -> p b t c", t=2)

        def split(ap):
            return ap.rearrange("p (b t) c -> p b t c", b=2)

        with nc.Block() as block:
            @block.sync
            def _(sp):
                def load_edge(g, slot):
                    e = s[f"edge{slot}"]
                    y = group_of(A["y"], g)
                    sp.dma_start(rbf[slot][:], group_of(A["rbf"], g)).then_inc(e, 16)
                    sp.dma_start(y_scal[slot][0:64, :], y[0, :].partition_broadcast(64)).then_inc(e, 16)
                    for x in range(3):
                        sp.dma_start(y_vec[slot][32 * x:32 * x + 32, :], y[x + 1, :].partition_broadcast(32)).then_inc(e, 16)
                    sp.dma_start(y_edge[slot][:], group_of(A["y_edge"], g)).then_inc(e, 16)

                def step(g, slot, use, now, before):
                    if now:
                        if not before:
                            load_edge(0, 0)
                        else:
                            wait_apart(sp, s["edge_value"], g, s["tick_s"])
                        load_edge(g + 1, 1 - slot)
                    if before:
                        window_rows(nc, sp, g - 1, window_from, K["least_i"], sums, st_in, st_out, s)

                sp.sem_inc(s["state_out"], 16)
                schedule(step)(sp)
                total = sp.value_load(window_from[0:1, NG:NG + 1], min_val=1, max_val=MAX_W)
                wait_apart(sp, s["state_out"], total * 16 + 16, s["tick_s"])
                sp.wait_ge(s["edge1"], loads * (NG // 2 + 1))

            @block.gpsimd
            def _(pool):
                def wait(sm, value):
                    wait_apart(pool, sm, value, s["tick"])

                def gather(g, slot, use, fresh):
                    if not fresh:
                        wait(s[f"got{slot}"], use * 64)
                    pool.tensor_copy(idx[slot][:], idx_all[:, bass.ds(g, 1), 0:TILES].rearrange("p a c -> p (a c)")).then_inc(s["indexed"], 1)
                    wait(s["indexed"], g + 1)
                    if not fresh:
                        wait(s["turned"], g - 1)
                    for t in range(TILES):
                        pool.indirect_dma_start(
                            out=got[slot][:, t, :], out_offset=None, in_=f_tab[:, :],
                            in_offset=bass.IndirectOffsetOnAxis(ap=idx[slot][:, t:t + 1], axis=0)
                        ).then_inc(s[f"got{slot}"], 16)

                def double(g, slot, use):
                    wait(s[f"got{slot}"], use * 64 + 64)
                    pool.tensor_copy(got2[slot][:].rearrange("p t (k c) -> p t k c", k=2),
                                     got[slot][:, :, 0:CS].unsqueeze(2).broadcast_to([P, TILES, 2, CS])).then_inc(s["doubled"], 1)

                def leave(g, slot, use, more):
                    if more:
                        gather(g + 2, slot, use + 1, False)
                    window_masks(pool, wait, g, K, s, None, dst_f, rel, first_node, to_node)
                    if more:
                        double(g + 2, slot, use + 1)

                pool.sem_inc(s["window_sum"], 1)
                for g in range(2):
                    gather(g, g, 0, True)
                    double(g, g, 0)
                with pool.Fori(0, NG // 2) as i:
                    leave(i * 2, 0, i, True)
                    leave(i * 2 + 1, 1, i, True)
                leave(NG - 1, 0, NG // 2, False)

            @block.tensor
            def _(pe):
                def step(g, slot, use, now, before):
                    if now:
                        pe.wait_ge(s[f"edge{slot}"], use * loads + loads)
                        if before:
                            pe.wait_ge(s["product"], g * 3 - 1)
                        nc.tensor.matmul(pW[0:64, 0:512], K["w_fc1"][:], rbf[slot][:], start=True, stop=True).then_inc(s["hidden_raw"], 1)
                        pe.wait_ge(s["doubled"], g + 1)
                        for t in range(TILES):
                            nc.tensor.transpose(pT[:, P * t:P * t + P], got2[slot][:, t, :], ident[:])
                            last = nc.tensor.transpose(pT[0:96, 512 + P * t:640 + P * t], got[slot][:, t, CS:D], ident[:])
                        last.then_inc(s["turned"], 1)
                    if now:
                        pe.wait_ge(s["hidden"], g + 1)
                        if before:
                            pe.wait_ge(s["product"], g * 3)
                        nc.tensor.matmul(pW[:, 512:1024], K["w_f01"][:], hid[:], start=True, stop=True).then_inc(s["weight"], 1)
                        nc.tensor.matmul(pW[0:96, 0:512], K["w_f3"][:], hid[:], start=True, stop=True).then_inc(s["weight"], 1)
                        pe.wait_ge(s["product"], g * 3 + 1)
                        nc.tensor.matmul(pW[0:96, 512:1024], K["w_f2"][:], hid[:], start=True, stop=True).then_inc(s["weight"], 1)
                        pe.wait_ge(s["scaled_product"], g * 2 + 2)
                        pe.wait_ge(s["product"], g * 3 + 3)
                        for t in range(TILES):
                            c = slice(P * t, P * t + P)
                            nc.tensor.matmul(edge_tile(t, 0, 97), prod[:, 0, c], K["w_c1"][:], start=True, stop=False)
                            nc.tensor.matmul(edge_tile(t, 0, 65), prod[0:96, 1, c], K["w_c2"][:], start=False, stop=False)
                            last = nc.tensor.matmul(edge_tile(t, 97, 193), prod[0:96, 2, c], K["w_c3"][:], start=False, stop=True)
                        last.then_inc(s["edge_sums"], 1)
                    if before:
                        w0, w1 = window_numbers(pe, window_from, g - 1)
                        pe.wait_ge(s["edge_value"], g)
                        pe.wait_ge(s["scal_copied"], g)
                        pe.sem_inc(s["tick"], 1)
                        with pe.Fori(w0, w1) as w:
                            pe.wait_ge(s["masks"], w + 1)
                            pe.wait_ge(s["merged"], w + 1)
                            for t in range(TILES):
                                last = nc.tensor.matmul(win, to_node[:, t, :], val[1 - slot][:, t, :], start=t == 0,
                                                        stop=t == TILES - 1)
                            last.then_inc(s["window_sum"], 1)
                schedule(step)(pe)

            @block.scalar
            def _(act):
                def step(g, slot, use, now, before):
                    if now:
                        act.wait_ge(s["hidden_raw"], g + 1)
                        nc.scalar.activation(th[:], pW[0:64, 0:512], ACT.Tanh, scale=0.125).then_inc(s["hid_tanh"], 1)
                        act.wait_ge(s["turned"], g + 1)
                        nc.scalar.activation(e0T[:], pT[:, 0:512], ACT.Copy)
                        nc.scalar.activation(e1T[:], pT[0:96, 512:1024], ACT.Copy).then_inc(s["turned_copied"], 1)
                        act.wait_ge(s["edge_sums"], g + 1)
                        act.wait_ge(s["ones"], 2)
                        nc.scalar.activation(split(val[slot][:, :, 0:65]), by_tile[:, :, :, 0:65], ACT.Copy).then_inc(s["scal_copied"], 1)
                schedule(step)(act)

            @block.vector
            def _(dve):
                def step(g, slot, use, now, before):
                    if now:
                        dve.wait_ge(s["hid_tanh"], g + 1)
                        dve.scalar_tensor_tensor(hid[:], th[:], 1.0, pW[0:64, 0:512], ALU.add, ALU.mult).then_inc(s["hidden"], 1)
                        dve.wait_ge(s[f"edge{slot}"], use * loads + loads)
                        dve.wait_ge(s["ones"], 2)
                        dve.wait_ge(s["turned_copied"], g + 1)
                        dve.wait_ge(s["weight"], g * 3 + 1)
                        dve.tensor_tensor(prod[:, 0, :], pW[:, 512:1024], e0T[:], ALU.mult).then_inc(s["product"], 1)
                        dve.wait_ge(s["weight"], g * 3 + 2)
                        dve.tensor_tensor(prod[0:96, 1, :], pW[0:96, 0:512], e1T[:], ALU.mult).then_inc(s["product"], 1)
                        dve.wait_ge(s["product"], g * 3 + 1)
                        dve.tensor_tensor(prod[:, 0, :], prod[:, 0, :], y_scal[slot][:], ALU.mult).then_inc(s["scaled_product"], 1)
                        dve.wait_ge(s["weight"], g * 3 + 3)
                        dve.tensor_tensor(prod[0:96, 2, :], pW[0:96, 512:1024], e1T[:], ALU.mult).then_inc(s["product"], 1)
                        dve.wait_ge(s["product"], g * 3 + 2)
                        dve.tensor_tensor(prod[0:96, 1, :], prod[0:96, 1, :], y_vec[slot][:], ALU.mult).then_inc(s["scaled_product"], 1)
                    if before:
                        w0, w1 = window_numbers(dve, window_from, g - 1)
                        with dve.Fori(w0, w1) as w:
                            dve.wait_ge(s["state_in"], w * 16 + 16)
                            dve.wait_ge(s["window_sum"], w + 2)
                            dve.tensor_tensor(st_out[:], st_in[:], win, ALU.add).then_inc(s["merged"], 1)
                    if now:
                        dve.wait_ge(s["edge_sums"], g + 1)
                        dve.wait_ge(s["scal_copied"], g + 1)
                        for t in range(0, TILES, 2):
                            o = by_tile[:, t // 2, :, :]
                            y = y_edge[slot][:, t:t + 2, :]
                            dve.tensor_tensor(vec[:, 0, t:t + 2, :], o[:, :, 97:193], y[:, :, 0:1].broadcast_to([P, 2, 96]), ALU.mult)
                            last = dve.tensor_tensor(vec[:, 1, t:t + 2, :].rearrange("p t (x d) -> p t x d", x=3),
                                                     o[:, :, 65:97].unsqueeze(2).broadcast_to([P, 2, 3, CV]),
                                                     y[:, :, 1:4].unsqueeze(3).broadcast_to([P, 2, 3, CV]), ALU.mult)
                        last.then_inc(s["vec_step"], 1)
                        dve.wait_ge(s["vec_step"], g + 1)
                        dve.tensor_tensor(val[slot][:, :, 65:161], vec[:, 0, :, :], vec[:, 1, :, :], ALU.add).then_inc(s["edge_value"], 1)
                for i in range(2):
                    dve.memset(y_scal[i][64:128, :], 1.0)
                    dve.memset(val[i][:, :, QW - 1:QW], 1.0).then_inc(s["ones"], 1)
                dve.sem_inc(s["merged"], 1)
                schedule(step)(dve)


def node2(nc, ctx, A, K, out):
    keep, sums, attr, chunk_rows = (K[n] for n in ("keep", "sums", "attr", "chunk_rows"))
    with ExitStack() as sx:
        def tmp(name, shape, dt=F32):
            return sx.enter_context(nc.sbuf_tensor(name, shape, dt))
        S = {n: ctx.enter_context(nc.semaphore("n2_" + n)) for n in ("x0", "x1", "ch", "res", "out0", "out1")}
        q = [tmp(f"q{i}", [P, CH, QW]) for i in range(2)]
        r = [tmp(f"r{i}", [P, CH, D]) for i in range(2)]
        f = tmp("f", [P, 4, CH])
        out_rows = out.rearrange("(c t p) f -> c p t f", t=CH, p=P)
        sum_rows = sums[0:NODES_PAD, :].rearrange("(c t p) f -> c p t f", t=CH, p=P)
        with nc.Block() as block:
            @block.sync
            def _(sp):
                for c in range(NCH):
                    if c >= 2:
                        sp.wait_ge(S["res"], c - 1)
                    sp.dma_start(q[c % 2][:], sum_rows[c]).then_inc(S[f"x{c % 2}"], 16)
                    if c >= 1:
                        sp.wait_ge(S["res"], c)
                        sp.dma_start(out_rows[c - 1], r[(c - 1) % 2][:]).then_inc(S[f"out{(c - 1) % 2}"], 16)
                sp.wait_ge(S["res"], NCH)
                sp.dma_start(out_rows[NCH - 1], r[(NCH - 1) % 2][:]).then_inc(S[f"out{(NCH - 1) % 2}"], 16)
                for i in range(2):
                    sp.wait_ge(S[f"out{i}"], 16 * ((NCH + 1 - i) // 2))

            @block.vector
            def _(dve):
                chain = Chain(dve, S["ch"], 6)
                for c in range(NCH):
                    chain.begin(c)
                    t = q[c % 2]
                    o = r[c % 2]
                    a = attr[:, c * CH:(c + 1) * CH]
                    k = keep[:, c * CH:(c + 1) * CH, :]
                    dve.wait_ge(S[f"x{c % 2}"], 16 * (c // 2) + 16)
                    chain.step(dve.tensor_scalar(f[:, 0, :], t[:, :, QW - 1], 1.0, None, ALU.max))
                    chain.step(dve.reciprocal(f[:, 1, :], f[:, 0, :]))
                    chain.step(dve.scalar_tensor_tensor(f[:, 2, :], f[:, 1, :], 1 / math.sqrt(96.0), a, ALU.mult, ALU.mult))
                    chain.step(dve.tensor_tensor(f[:, 3, :], f[:, 2, :], t[:, :, CS], ALU.mult))
                    chain.step(dve.tensor_tensor(f[:, 3, :], f[:, 3, :], f[:, 2, :], ALU.mult))
                    by = f[:, 3, :].unsqueeze(2)
                    dve.tensor_tensor(t[:, :, 0:CS], t[:, :, 0:CS], by.broadcast_to([P, CH, CS]), ALU.mult)
                    chain.step(dve.tensor_tensor(t[:, :, CS + 1:QW - 1], t[:, :, CS + 1:QW - 1], by.broadcast_to([P, CH, 96]), ALU.mult))
                    if c >= 2:
                        dve.wait_ge(S[f"out{c % 2}"], 16 * (c // 2))
                    dve.tensor_tensor(o[:, :, 0:CS], t[:, :, 0:CS], k[:, :, 0:CS], ALU.add)
                    for x in range(3):
                        last = dve.tensor_tensor(o[:, :, CS + x:D:3], t[:, :, CS + 1 + CV * x:CS + 1 + CV * x + CV], k[:, :, CS + x:D:3], ALU.add)
                    last.then_inc(S["res"], 1)
                    chain.end()


def kernel(**inputs):
    import concourse.bacc as bacc
    from concourse.bass_utils import run_bass_kernel_spmd

    a = {n: np.asarray(v) for n, v in inputs.items()}
    pad_e = NG_PAD * GE - N_EDGES
    src = np.pad(a["src"], (0, pad_e)).reshape(NG_PAD, TILES, P)
    dst = np.pad(a["dst"], (0, pad_e), constant_values=N_NODES).reshape(NG_PAD, TILES, P)
    y = np.pad(a["edge_attr_4"], ((0, pad_e), (0, 0)))
    arrays = {
        "x": np.pad(a["x"], ((0, NODES_PAD - N_NODES), (0, 0))),
        "node_attr": np.pad(a["node_vec1"][:, 0], (0, NODES_PAD - N_NODES)).reshape(NT, P).T,
        "idx": np.concatenate([src, dst], axis=1).transpose(0, 2, 1),
        "dst_rows": dst.reshape(NG_PAD, GE),
        "rbf": np.pad(a["edge_attr_16"], ((0, pad_e), (0, 0))).reshape(NG_PAD, GE, NB).transpose(0, 2, 1),
        "y": y.reshape(NG_PAD, GE, 4).transpose(0, 2, 1),
        "y_edge": y.reshape(NG_PAD, TILES, P, 4).transpose(0, 2, 1, 3),
        "Ws_val_t": a["L0_gnn_Ws_val"].T,
        "alpha_dot": a["L0_gnn_alpha_dot"].reshape(-1),
    }
    for n in ("gamma_s", "beta_s", "gamma_v", "Ws_src", "Wv_src", "Ws_dst", "Wv_dst", "W_rbf", "W_alpha", "Ws_val",
              "Wv_val", "Wg", "Ws_vlin", "Wv_vlin", "Wps", "Wpv"):
        arrays[n] = a["L0_gnn_" + n]
    for n in ("w2_ss", "w2_sv", "w2_vs", "w2_vv0", "w2_vv1"):
        arrays[n] = a["L0_gnn_" + n].reshape(-1, 1)
    for n in ("Wfc1", "Wfc2", "Wsc0", "Wsc1", "Wl1_0", "Wl1_1", "Wl2_s", "Wl2_v", "Wa"):
        arrays[n] = a["L1_gnn_" + n]
    arrays = {"in_" + n: np.ascontiguousarray(v) for n, v in arrays.items()}
    nc = bacc.Bacc("TRN2", target_bir_lowering=False, num_devices=1)
    ins = {n[3:]: nc.dram_tensor(n, v.shape, mybir.dt.from_np(v.dtype), kind="ExternalInput").ap() for n, v in arrays.items()}
    out = nc.dram_tensor("out", (NODES_PAD, D), F32, kind="ExternalOutput").ap()
    build(nc, ins, out)
    return run_bass_kernel_spmd(nc, [arrays], core_ids=[0]).results[0]["out"][:N_NODES]
```

```python
import math
from contextlib import ExitStack

import numpy as np
import concourse.bass as bass
from concourse import mybir

F32 = mybir.dt.float32
I32 = mybir.dt.int32
ALU = mybir.AluOpType
ACT = mybir.ActivationFunctionType
AX = mybir.AxisListType

P = 128
N_NODES, N_EDGES = 6250, 200000
CS, CV, NB, HEADS, AS, AV = 64, 32, 16, 4, 16, 8
D = CS + 3 * CV
TILES = 4
GE = TILES * P
NG = -(-N_EDGES // GE)
NG_PAD = 392
GROUP_ROWS = 98
NT = -(-N_NODES // P)
CH = 7
NCH = NT // CH
NODES_PAD = NT * P
STATE_ROWS = 50 * P
HW = 1 + AS + 3 * AV
SW = HEADS * (1 + HW)
QW = CS + 1 + 3 * CV + 1
LEAST = -1e30
EPS = 1e-5
R2, R3 = 1 / math.sqrt(2.0), 1 / math.sqrt(3.0)
MAX_W = 50 * NG_PAD


class Chain:

    def __init__(self, eng, sem, per_round):
        self.eng, self.sem, self.per, self.base, self.k = eng, sem, per_round, 0, 0

    def begin(self, round_):
        self.base, self.k = round_ * self.per, 0

    def end(self):
        assert self.k == self.per, self.k

    def step(self, instruction):
        self.k += 1
        instruction.then_inc(self.sem, 1)
        self.eng.wait_ge(self.sem, self.base + self.k)


def wait_apart(eng, sem, value, tick):
    eng.wait_ge(sem, value)
    eng.sem_inc(tick, 1)


def build(nc, ins, out):
    ctx = ExitStack()
    with ctx:
        ctx.enter_context(nc.allow_non_contiguous_dma(reason="small tables, once"))
        program(nc, ctx, ins, out)


def program(nc, ctx, A, out):
    def sb(name, shape, dt=F32):
        return ctx.enter_context(nc.sbuf_tensor(name, shape, dt))

    def sem(name):
        return ctx.enter_context(nc.semaphore(name))

    def dram(name, shape, dt=F32):
        return nc.dram_tensor(name, shape, dt, kind="Internal").ap()

    src_tab = dram("src_tab", (NODES_PAD, D))
    dst_tab = dram("dst_tab", (NODES_PAD, D))
    f_tab = dram("f_tab", (NODES_PAD, CS + D))
    state = dram("state", (STATE_ROWS, SW))
    sums = dram("sums", (STATE_ROWS, QW))
    group_dram = dram("group_dram", (2, NG_PAD))

    ident = sb("ident", [P, P])
    iota_row = sb("iota_row", [P, P])
    iota_col = sb("iota_col", [P, 1])
    least_bc = sb("least_bc", [P, NG_PAD])
    window_from = sb("window_from", [1, NG_PAD + 8], I32)
    least_i = sb("least_i", [1, NG_PAD], I32)
    idx_all = sb("idx_all", [P, NG_PAD, 2 * TILES], I32)
    keep = sb("keep", [P, NT, D])
    w_edge = sb("w_edge", [64, 6, P])
    w_msg = sb("w_msg", [P, 6, 256])
    w_val = sb("w_val", [P, 5, D])
    adot = sb("adot", [P, HEADS * AS])
    gam_s = sb("gam_s", [P, CS])
    bet_s = sb("bet_s", [P, CS])
    gam_v = sb("gam_v", [P, CV])
    w_n0s = sb("w_n0s", [64, 2 * CS])
    w_n0v = sb("w_n0v", [96, 6 * CV])
    w_n1s = sb("w_n1s", [64, 2 * CS])
    w_n1v = sb("w_n1v", [96, 6 * CV])
    w_out_a = sb("w_out_a", [P, D])
    w_out_b = sb("w_out_b", [CV, D])
    w_fc1 = sb("w_fc1", [NB, 64])
    w_f01 = sb("w_f01", [64, P])
    w_f3 = sb("w_f3", [64, 96])
    w_f2 = sb("w_f2", [64, 96])
    w_c1 = sb("w_c1", [P, 97])
    w_c2 = sb("w_c2", [96, 65])
    w_c3 = sb("w_c3", [96, 96])
    attr = sb("attr", [P, NT])

    psum = [ctx.enter_context(nc.psum_tensor(f"bank_pair_{i}", [P, 1024], F32)) for i in range(4)]

    def heads(ap):
        return ap.rearrange("p (h c) -> p h c", h=HEADS)

    with ExitStack() as sx:
        def tmp(name, shape, dt=F32):
            return sx.enter_context(nc.sbuf_tensor(name, shape, dt))

        s_zero, s_load, s_ident, s_scale, s_gate, s_gatec = (sem(n) for n in (
            "s_zero", "s_load", "s_ident", "s_scale", "s_gate", "s_gatec"))
        s_dst, s_ext, s_extw, s_row, s_sc, s_init, s_initd, s_meta = (sem(n) for n in (
            "s_dst", "s_ext", "s_extw", "s_row", "s_sc", "s_init", "s_initd", "s_meta"))
        val_t = tmp("val_t", [CS, CS + 3 * CV])
        wg = tmp("wg", [CS, CV])
        scale5 = tmp("scale5", [P, 5])
        fac5 = tmp("fac5", [P, 5])
        dst_g = tmp("dst_g", [GROUP_ROWS, NG_PAD // GROUP_ROWS, GE], I32)
        ext_i = tmp("ext_i", [GROUP_ROWS, 2, NG_PAD // GROUP_ROWS])
        row = tmp("row", [1, 2, NG_PAD])
        cnt_f = tmp("cnt_f", [1, NG_PAD])
        cnt_i = tmp("cnt_i", [1, NG_PAD], I32)
        scan_a = tmp("scan_a", [1, NG_PAD])
        scan_b = tmp("scan_b", [1, NG_PAD])
        init_state = tmp("init_state", [P, 10, SW])
        iota_i = tmp("iota_i", [P, P], I32)
        iota_ci = tmp("iota_ci", [P, 1], I32)
        n_load = [0]

        with nc.Block() as block:
            @block.sync
            def _(sp):
                sp.dma_start(dst_g[:], A["dst_rows"].rearrange("(c p) e -> p c e", p=GROUP_ROWS)).then_inc(s_dst, 16)
                sp.wait_ge(s_zero, 1)

                def put(to, frm):
                    sp.dma_start(to, frm).then_inc(s_load, 16)
                    n_load[0] += 16

                put(idx_all[:], A["idx"].rearrange("g p c -> p g c"))
                put(adot[:], A["alpha_dot"].partition_broadcast(P))
                put(gam_s[:], A["gamma_s"].partition_broadcast(P))
                put(bet_s[:], A["beta_s"].partition_broadcast(P))
                put(gam_v[:], A["gamma_v"].partition_broadcast(P))
                put(attr[:], A["node_attr"])
                Wr = A["W_rbf"]
                o_ss, o_sv, o_vs, o_vv0, o_vv1 = 0, CS, 2 * CS, 2 * CS + CV, 2 * CS + 2 * CV

                def edge_rows(k):
                    return slice(NB * k, NB * k + NB)

                put(w_edge[edge_rows(0), 0, 0:64], Wr[:, o_ss:o_ss + 64])
                put(w_edge[edge_rows(1), 0, 64:128], Wr[:, o_sv:o_sv + 64])
                put(w_edge[edge_rows(2), 1, 0:64], Wr[:, o_sv:o_sv + 64])
                put(w_edge[edge_rows(3), 1, 64:128], Wr[:, o_sv:o_sv + 64])
                for j in range(3):
                    c = slice(32 * j, 32 * j + 32)
                    put(w_edge[edge_rows(j + 1), 2, c], Wr[:, o_vv0:o_vv0 + 32])
                    put(w_edge[edge_rows(0), 3, c], Wr[:, o_vs:o_vs + 32])
                    put(w_edge[edge_rows((j + 1) % 3 + 1), 4, c], Wr[:, o_vv1:o_vv1 + 32])
                    put(w_edge[edge_rows((j + 2) % 3 + 1), 5, c], Wr[:, o_vv1:o_vv1 + 32])
                Wa, Ws, Wv = A["W_alpha"], A["Ws_val"], A["Wv_val"]
                put(w_msg[0:64, 0, 96:160], Ws[0:64, :])
                put(w_msg[0:64, 0, 192:256], Wa[0:64, :])
                put(w_msg[64:128, 0, 0:32], Wv[0:64, :])
                put(w_msg[0:64, 1, 32:64], Wv[0:64, :])
                put(w_msg[64:128, 1, 64:96], Wv[0:64, :])
                for j in range(3):
                    r = slice(32 * j, 32 * j + 32)
                    u, w = 32 * ((j + 2) % 3), 32 * ((j + 1) % 3)
                    put(w_msg[r, 2, 96:160], Ws[64:96, :])
                    put(w_msg[r, 2, 192:256], Wa[64:96, :])
                    put(w_msg[r, 3, r], Wv[64:96, :])
                    put(w_msg[r, 4, u:u + 32], Wv[96:128, :])
                    put(w_msg[r, 5, w:w + 32], Wv[96:128, :])
                put(val_t[:, 0:64], A["Ws_val_t"][:, 0:64])
                for j in range(3):
                    put(val_t[:, 64 + 32 * j:96 + 32 * j], A["Ws_val_t"][:, 64:96])
                put(wg[:], A["Wg"])
                for b, r, _, source, first, axis, vec, vfirst in value_pieces():
                    to = heads(w_val[r:r + 32, b, :])
                    frm = A[source][first:first + 32, :]
                    if axis is None:
                        put(to[:, :, 0:AS], frm.rearrange("p (h c) -> p h c", h=HEADS))
                    else:
                        put(to[:, :, AS + AV * axis:AS + AV * axis + AV], frm.rearrange("p (h c) -> p h c", h=HEADS))
                    put(scale5[r:r + 32, b:b + 1], A[vec][vfirst:vfirst + 32, :])
                put(w_n0s[:, 0:64], A["Ws_src"])
                put(w_n0s[:, 64:128], A["Ws_dst"])
                put(w_n1s[:, 0:64], A["Wl1_0"])
                put(w_n1s[:, 64:128], A["Wsc0"])
                for j in range(3):
                    r = slice(32 * j, 32 * j + 32)
                    q = slice(96 + 32 * j, 128 + 32 * j)
                    put(w_n0v[r, r], A["Wv_src"])
                    put(w_n0v[r, q], A["Wv_dst"])
                    put(w_n1v[r, r], A["Wl1_1"])
                    put(w_n1v[r, q], A["Wsc1"])
                for h in range(HEADS):
                    rows = [(40 * h, AS, A["Wps"][AS * h:AS * h + AS, :], 0)]
                    rows += [(40 * h + AS + AV * x, AV, A["Wpv"][AV * h:AV * h + AV, :], CS + CV * x) for x in range(3)]
                    for r, n, frm, c in rows:
                        cut = min(max(P - r, 0), n)
                        width = frm.shape[1]
                        if cut:
                            put(w_out_a[r:r + cut, c:c + width], frm[0:cut, :])
                        if cut < n:
                            put(w_out_b[r + cut - P:r + n - P, c:c + width], frm[cut:n, :])
                put(w_fc1[:], A["Wfc1"])
                put(w_f01[:], A["Wfc2"][:, 0:128])
                put(w_c1[0:64, 0:64], A["Wl2_s"][0:64, :])
                put(w_c1[0:64, 64:65], A["Wa"][0:64, :])
                put(w_c1[64:128, 65:97], A["Wl2_v"][0:64, :])
                for j in range(3):
                    r = slice(32 * j, 32 * j + 32)
                    put(w_f3[:, r], A["Wfc2"][:, 160:192])
                    put(w_f2[:, r], A["Wfc2"][:, 128:160])
                    put(w_c2[r, 0:64], A["Wl2_s"][64:96, :])
                    put(w_c2[r, 64:65], A["Wa"][64:96, :])
                    put(w_c3[r, r], A["Wl2_v"][64:96, :])
                sp.wait_ge(s_ext, 2)
                for k in range(2):
                    sp.dma_start(group_dram[k, :].rearrange("(c p) -> p c", p=GROUP_ROWS), ext_i[:, k, :]).then_inc(s_extw, 16)
                sp.wait_ge(s_extw, 32)
                sp.dma_start(row[:], group_dram.rearrange("k g -> (k g)").unsqueeze(0).rearrange("o (k g) -> o k g", k=2)).then_inc(s_row, 16)
                sp.dma_start(least_bc[:], group_dram[0, :].partition_broadcast(P)).then_inc(s_meta, 16)
                sp.wait_ge(s_init, 1)
                for i in range(5):
                    sp.dma_start(state[i * 10 * P:(i + 1) * 10 * P, :].rearrange("(a p) c -> p a c", p=P), init_state[:]).then_inc(s_initd, 16)
                    sp.dma_start(sums[i * 10 * P:(i + 1) * 10 * P, :].rearrange("(a p) c -> p a c", p=P), init_state[:, :, 4:4 + QW]).then_inc(s_initd, 16)
                sp.wait_ge(s_initd, 160)
                sp.wait_ge(s_meta, 16)
                sp.wait_ge(s_load, n_load[0])

            @block.gpsimd
            def _(pool):
                pool.memset(ident[:], 0.0).then_inc(s_ident, 1)
                pool.iota(iota_i[:], [[1, P]], base=0, channel_multiplier=0).then_inc(s_ident, 1)
                pool.iota(iota_ci[:], [[1, 1]], base=0, channel_multiplier=1).then_inc(s_ident, 1)
                pool.wait_ge(s_ident, 3)
                pool.affine_select(out=ident[:], in_=ident[:], compare_op=ALU.not_equal, fill=1.0, base=0,
                                   pattern=[[-1, P]], channel_multiplier=1).then_inc(s_ident, 1)
                pool.tensor_copy(iota_row[:], iota_i[:]).then_inc(s_ident, 1)
                pool.tensor_copy(iota_col[:], iota_ci[:]).then_inc(s_ident, 1)

            @block.tensor
            def _(pe):
                pe.wait_ge(s_load, n_load[0])
                nc.tensor.matmul(psum[0][0:64, 0:32], val_t[:, 0:64], wg[:], start=True, stop=True)
                nc.tensor.matmul(psum[0][0:96, 512:544], val_t[:, 64:160], wg[:], start=True, stop=True).then_inc(s_gate, 1)

            @block.vector
            def _(dve):
                for t in (w_edge, w_msg, w_val, w_n0v, w_n1v, w_out_a, w_out_b, w_c1, w_c3):
                    last = dve.memset(t[:], 0.0)
                last.then_inc(s_zero, 1)
                dve.memset(init_state[:, :, 4:SW], 0.0)
                dve.memset(init_state[:, :, 0:4], LEAST).then_inc(s_init, 1)
                for b, r, factor, *_ in value_pieces():
                    last = dve.memset(fac5[r:r + 32, b:b + 1], 0.5 * factor)
                last.then_inc(s_scale, 1)
                dve.wait_ge(s_dst, 16)
                dve.tensor_reduce(ext_i[:, 0, :], dst_g[:], axis=AX.X, op=ALU.min).then_inc(s_ext, 1)
                dve.tensor_reduce(ext_i[:, 1, :], dst_g[:], axis=AX.X, op=ALU.max).then_inc(s_ext, 1)
                dve.wait_ge(s_row, 16)
                chain = Chain(dve, s_sc, 99)
                chain.step(dve.tensor_tensor(cnt_f[:], row[:, 1, :], row[:, 0, :], ALU.subtract))
                chain.step(dve.tensor_copy(cnt_i[:], cnt_f[:]))
                chain.step(dve.tensor_scalar(cnt_i[:], cnt_i[:], 7, None, ALU.logical_shift_right))
                chain.step(dve.tensor_copy(scan_a[:], cnt_i[:]))
                chain.step(dve.tensor_scalar(scan_a[:], scan_a[:], 1.0, None, ALU.add))
                a, b, d = scan_a, scan_b, 1
                while d < NG_PAD:
                    dve.tensor_copy(b[:, 0:d], a[:, 0:d])
                    chain.step(dve.tensor_tensor(b[:, d:NG_PAD], a[:, d:NG_PAD], a[:, 0:NG_PAD - d], ALU.add))
                    a, b, d = b, a, 2 * d
                chain.step(dve.memset(window_from[:], 0))
                dve.tensor_copy(least_i[:], row[:, 0, :])
                chain.step(dve.tensor_copy(window_from[:, 1:NG_PAD + 1], a[:]))
                dve.wait_ge(s_load, n_load[0])
                dve.wait_ge(s_gate, 1)
                dve.tensor_copy(w_msg[0:64, 0, 160:192], psum[0][0:64, 0:32])
                chain.step(dve.tensor_copy(w_msg[0:96, 2, 160:192], psum[0][0:96, 512:544]))
                dve.tensor_scalar(w_msg[0:96, 2, 96:256], w_msg[0:96, 2, 96:256], R3, None, ALU.mult)
                dve.tensor_scalar(w_msg[0:96, 4, 0:96], w_msg[0:96, 4, 0:96], R2, None, ALU.mult)
                dve.tensor_scalar(w_msg[0:96, 5, 0:96], w_msg[0:96, 5, 0:96], -R2, None, ALU.mult)
                dve.tensor_scalar(w_n1s[:], w_n1s[:], 1 / math.sqrt(64.0), None, ALU.mult)
                dve.tensor_scalar(w_n1v[:], w_n1v[:], 1 / math.sqrt(32.0), None, ALU.mult)
                dve.tensor_scalar(w_c1[:], w_c1[:], 1 / 64.0, None, ALU.mult)
                dve.tensor_scalar(w_c2[:], w_c2[:], R3 / 64.0, None, ALU.mult)
                dve.tensor_scalar(w_c3[:], w_c3[:], 1 / 64.0, None, ALU.mult)
                chain.step(dve.tensor_tensor(scale5[:], scale5[:], fac5[:], ALU.mult))
                for k in range(5):
                    last = dve.tensor_scalar(w_val[:, k, :], w_val[:, k, :], scale5[:, k:k + 1], None, ALU.mult)
                chain.step(last)

    def normalize(dve, chain, x, hid, stats, s_var, s_std, turn):
        n = x.shape[2]
        big = [P, CH, n]
        chain.step(dve.tensor_reduce(stats[:, 0, :], x, axis=AX.X, op=ALU.add))
        chain.step(dve.tensor_scalar(stats[:, 0, :], stats[:, 0, :], 1.0 / n, None, ALU.mult))
        chain.step(dve.tensor_tensor(hid[0], x, stats[:, 0, :].unsqueeze(2).broadcast_to(big), ALU.subtract))
        chain.step(dve.tensor_tensor(hid[1], hid[0], hid[0], ALU.mult))
        chain.step(dve.tensor_reduce(stats[:, 1, :], hid[1], axis=AX.X, op=ALU.add))
        dve.tensor_scalar(stats[:, 1, :], stats[:, 1, :], 1.0 / n, EPS, ALU.mult, ALU.add).then_inc(s_var, 1)
        dve.wait_ge(s_std, turn)
        chain.step(dve.reciprocal(stats[:, 2, :], stats[:, 1, :]))

    def project_pe(pe, it, node, w_s, w_v, S):
        for t in range(CH):
            if t == 0:
                pe.wait_ge(S["node"], it + 1)
            nc.tensor.transpose(psum[1][0:96, t * P:(t + 1) * P], node[:, t, CS:D], ident[:])
            last = nc.tensor.transpose(psum[0][0:64, t * P:(t + 1) * P], node[:, t, 0:CS], ident[:])
        last.then_inc(S["tr"], 1)
        pe.wait_ge(S["trc"], it + 1)
        for t in range(CH):
            bank = psum[2 + t % 2]
            if t >= 2:
                pe.wait_ge(S["pjc"], it * CH + t - 1)
            nc.tensor.matmul(bank[:, 0:128], S["nts"][:, t * P:(t + 1) * P], w_s[:], start=True, stop=True)
            nc.tensor.matmul(bank[:, 512:704], S["ntv"][:, t * P:(t + 1) * P], w_v[:], start=True,
                             stop=True).then_inc(S["pj"], 1)

    def project_act(act, it, both, S):
        act.wait_ge(S["tr"], it + 1)
        nc.scalar.activation(S["nts"][:], psum[0][0:64, 0:CH * P], ACT.Copy)
        nc.scalar.activation(S["ntv"][:], psum[1][0:96, 0:CH * P], ACT.Copy).then_inc(S["trc"], 1)
        for t in range(CH):
            bank = psum[2 + t % 2]
            act.wait_ge(S["pj"], it * CH + t + 1)
            o = both[:, :, t, :]
            nc.scalar.activation(o[:, :, 0:CS], bank[:, 0:128].rearrange("p (k c) -> p k c", k=2), ACT.Copy)
            nc.scalar.activation(o[:, :, CS:D], bank[:, 512:704].rearrange("p (k c) -> p k c", k=2),
                                 ACT.Copy).then_inc(S["pjc"], 1)

    def chunk_rows(table, it):
        return table.rearrange("(c t p) f -> c p t f", t=CH, p=P)[bass.ds(it, 1), :, :, :].rearrange("c p t f -> (c p) t f")

    with ExitStack() as sx:
        def tmp(name, shape, dt=F32):
            return sx.enter_context(nc.sbuf_tensor(name, shape, dt))
        x_in = tmp("x_in", [P, CH, D])
        cen = tmp("cen", [P, CH, D])
        sq = tmp("sq", [P, CH, D])
        hn = tmp("hn", [P, CH, D])
        node = tmp("node", [P, CH, D])
        both = tmp("both", [P, 2, CH, D])
        stats = tmp("stats", [P, 3, CH])
        S = {n: sem("n0_" + n) for n in ("x", "var", "std", "node", "tr", "trc", "pj", "pjc", "ch", "tick", "out")}
        S["nts"] = tmp("nts", [64, CH * P])
        S["ntv"] = tmp("ntv", [96, CH * P])

        with nc.Block() as block:
            @block.sync
            def _(sp):
                with sp.Fori(0, NCH) as it:
                    sp.dma_start(x_in[:], chunk_rows(A["x"], it)).then_inc(S["x"], 16)
                    sp.wait_ge(S["pjc"], it * CH + CH)
                    for k, table in enumerate((src_tab, dst_tab)):
                        sp.dma_start(chunk_rows(table, it), both[:, k, :, :]).then_inc(S["out"], 16)
                    wait_apart(sp, S["out"], it * 32 + 32, S["tick"])

            @block.vector
            def _(dve):
                chain = Chain(dve, S["ch"], 22)
                with dve.Fori(0, NCH) as it:
                    chain.begin(it)
                    dve.wait_ge(S["x"], it * 16 + 16)
                    normalize(dve, chain, x_in[:], (cen[:], sq[:]), stats, S["var"], S["std"], it * 3 + 1)
                    chain.step(dve.tensor_tensor(cen[:], cen[:], stats[:, 2, :].unsqueeze(2).broadcast_to([P, CH, D]), ALU.mult))
                    chain.step(dve.tensor_scalar(hn[:], cen[:], 0.0, None, ALU.max))
                    chain.step(dve.tensor_tensor(keep[:, bass.ds(it * CH, CH), :], x_in[:], hn[:], ALU.add))
                    s, v = hn[:, :, 0:CS], hn[:, :, CS:D]
                    normalize(dve, chain, s, (cen[:, :, 0:CS], sq[:, :, 0:CS]), stats, S["var"], S["std"], it * 3 + 2)
                    small = [P, CH, CS]
                    chain.step(dve.tensor_tensor(cen[:, :, 0:CS], cen[:, :, 0:CS], stats[:, 2, :].unsqueeze(2).broadcast_to(small), ALU.mult))
                    chain.step(dve.tensor_tensor(cen[:, :, 0:CS], cen[:, :, 0:CS], gam_s[:].unsqueeze(1).broadcast_to(small), ALU.mult))
                    chain.step(dve.tensor_tensor(node[:, :, 0:CS], cen[:, :, 0:CS], bet_s[:].unsqueeze(1).broadcast_to(small), ALU.add))
                    chain.step(dve.tensor_tensor(sq[:, :, CS:D], v, v, ALU.mult))
                    chain.step(dve.tensor_reduce(stats[:, 1, :], sq[:, :, CS:D], axis=AX.X, op=ALU.add))
                    dve.tensor_scalar(stats[:, 1, :], stats[:, 1, :], 1.0 / CV, EPS, ALU.mult, ALU.add).then_inc(S["var"], 1)
                    dve.wait_ge(S["std"], it * 3 + 3)
                    chain.step(dve.reciprocal(stats[:, 2, :], stats[:, 1, :]))
                    chain.step(dve.tensor_tensor(cen[:, :, CS:D], v, stats[:, 2, :].unsqueeze(2).broadcast_to([P, CH, 3 * CV]), ALU.mult))
                    for x in range(3):
                        last = dve.tensor_tensor(node[:, :, CS + CV * x:CS + CV * x + CV], cen[:, :, CS + x:D:3],
                                                 gam_v[:].unsqueeze(1).broadcast_to([P, CH, CV]), ALU.mult)
                    last.then_inc(S["node"], 1)
                    chain.end()
            @block.scalar
            def _(act):
                with act.Fori(0, NCH) as it:
                    for k in range(3):
                        act.wait_ge(S["var"], it * 3 + k + 1)
                        nc.scalar.activation(stats[:, 1, :], stats[:, 1, :], ACT.Sqrt).then_inc(S["std"], 1)
                    project_act(act, it, both, S)

            @block.tensor
            def _(pe):
                with pe.Fori(0, NCH) as it:
                    project_pe(pe, it, node, w_n0s, w_n0v, S)


    layer0(nc, ctx, A, locals())
    node1(nc, ctx, A, locals())
    layer1(nc, ctx, A, locals())
    node2(nc, ctx, A, locals(), out)


def value_pieces():
    out = []
    for k in range(4):
        for j in range(3):
            r = 32 * j
            if k == 0:
                out.append((0, r, 1.0, "Wv_vlin", 64, j, "w2_vs", 0))
            elif j == k - 1:
                out.append((k, r, R3, "Ws_vlin", 64, None, "w2_vv0", 0))
            elif k - 1 == (j + 1) % 3:
                out.append((k, r, R2, "Wv_vlin", 96, (j + 2) % 3, "w2_vv1", 0))
            else:
                out.append((k, r, -R2, "Wv_vlin", 96, (j + 1) % 3, "w2_vv1", 0))
        for b, r, first in ((k, 96, 0), (4, 32 * k, 32)):
            if k == 0:
                out.append((b, r, 1.0, "Ws_vlin", first, None, "w2_ss", first))
            else:
                out.append((b, r, 1.0, "Wv_vlin", first, k - 1, "w2_sv", first))
    return out


def first_window(eng, window_from, g):
    at = slice(g, g + 1) if isinstance(g, int) else bass.ds(g, 1)
    return eng.value_load(window_from[0:1, at], min_val=0, max_val=MAX_W)


def more_windows(eng, first, end, body):
    with eng.If(first + 1 < end):
        with eng.Fori(first + 1, end) as w:
            body(w)


def schedule(step):
    def run(eng):
        step(0, 0, 0, True, False, False)
        step(1, 1, 0, True, True, False)
        with eng.Fori(1, NG // 2) as i:
            step(i * 2, 0, i, True, True, True)
            step(i * 2 + 1, 1, i, True, True, True)
        for g in range(NG // 2 * 2, NG):
            step(g, g % 2, g // 2, True, True, True)
        step(NG, NG % 2, NG // 2, False, True, True)
        step(NG + 1, (NG + 1) % 2, (NG + 1) // 2, False, False, True)
    return run


def mid_use(slot, use):
    return use if slot == 1 else use - 1


def group_of(ap, g):
    return ap[g] if isinstance(g, int) else ap[bass.ds(g, 1)].squeeze(0)

def layer0(nc, ctx, A, K):
    (ident, iota_row, iota_col, least_bc, window_from, idx_all, w_edge, w_msg, w_val, adot, psum, state,
     src_tab, dst_tab) = (K[n] for n in (
        "ident", "iota_row", "iota_col", "least_bc", "window_from", "idx_all", "w_edge", "w_msg", "w_val",
        "adot", "psum", "state", "src_tab", "dst_tab"))
    s = {n: ctx.enter_context(nc.semaphore("l0_" + n)) for n in (
        "edge0", "edge1", "wide0", "wide1", "got0", "got1", "summed", "scaled", "turned", "turned_copied",
        "logit_turned", "logit_copied", "value_turned", "weighted", "block_done", "message", "tanh", "relu",
        "gated", "gate", "logit", "logit_step", "value_block", "value", "top", "top_at_edge", "top_read", "far",
        "shifted", "expd", "value_scaled", "rescale", "factors", "window_sum", "merged", "win_step", "dst0", "dst1",
        "state_in", "state_out", "tick", "tick_v", "tick_s", "indexed", "scalars", "at_node", "first_masks",
        "dst_taken", "related", "more_at", "more_masks", "more_dst", "more_step")}
    heads = K["heads"]
    with ExitStack() as sx:
        def tmp(name, shape, dt=F32):
            return sx.enter_context(nc.sbuf_tensor(name, shape, dt))
        idx = [tmp(f"idx{i}", [P, 2 * TILES], I32) for i in range(2)]
        got_src = [tmp(f"got_src{i}", [P, TILES, D]) for i in range(2)]
        got_dst = [tmp(f"got_dst{i}", [P, TILES, D]) for i in range(2)]
        msg = [tmp(f"msg{i}", [P, TILES, CS + D]) for i in range(2)]
        rbf4 = [tmp(f"rbf4{i}", [64, GE]) for i in range(2)]
        y16 = [tmp(f"y16{i}", [64, GE]) for i in range(2)]
        edge = [tmp(f"edge{i}", [64, GE]) for i in range(2)]
        y_all = [tmp(f"y_all{i}", [P, 4, GE]) for i in range(2)]
        y_quad = [tmp(f"y_quad{i}", [P, GE]) for i in range(2)]
        dst_bc = [tmp(f"dst_bc{i}", [P, GE], I32) for i in range(2)]
        sT2 = tmp("sT2", [P, GE])
        vT = tmp("vT", [96, GE])
        blocks = tmp("blocks", [P, 6, GE])
        th = tmp("th", [P, TILES, 96])
        rl = tmp("rl", [P, TILES, 64])
        lg = tmp("lg", [P, TILES, 64])
        gated = [tmp(f"gated{i}", [P, TILES, 256]) for i in range(2)]
        gates = tmp("gates", [P, TILES, CV])
        logits = [tmp(f"logits{i}", [P, TILES * HEADS]) for i in range(2)]
        logit_bc = [tmp(f"logit_bc{i}", [P, HEADS, GE]) for i in range(2)]
        vblocks = tmp("vblocks", [P, 5, GE])
        far = tmp("far", [P, GE])
        at_node = [tmp(f"at_node{i}", [P, GE]) for i in range(2)]
        to_node = [tmp(f"to_node{i}", [P, TILES, P]) for i in range(2)]
        M = {"at_node": at_node, "to_node": to_node, "iota_row": iota_row, "dst_more": tmp("dst_more", [P, GE], I32),
             "dst_f": tmp("dst_f", [P, TILES]),
             "rel": tmp("rel", [P, TILES]),
             "first_node": tmp("first_node", [P, 1]),
             "down": tmp("down", [P, 1])}
        junk = tmp("junk", [P, HEADS, GE], mybir.dt.bfloat16)
        top = tmp("top", [P, HEADS])
        shift = tmp("shift", [P, TILES * HEADS])
        vals = tmp("vals", [P, TILES * HEADS, HW])
        st_in = tmp("st_in", [P, SW])
        st_out = tmp("st_out", [P, SW])
        diff = tmp("diff", [P, 2 * HEADS])
        fac = tmp("fac", [P, 2 * HEADS])
        part = tmp("part", [P, 2, HEADS * HW])

        pT, pW, pM, pV = psum
        messages = pM[:].rearrange("p (t c) -> p t c", t=TILES)
        def value_tile(t):
            o = 512 * (t // 2) + D * (t % 2)
            return pV[:, o:o + D]
        win = pV[:, 320:320 + HEADS * HW]
        top_edge = pV[:, 512 + 320:512 + 320 + TILES * HEADS]
        ebank = lambda b: pW[:, 512 * (b % 2):512 * (b % 2) + 512]

        with nc.Block() as block:
            @block.sync
            def _(sp):
                def load_edge(g, slot):
                    for k in range(4):
                        rows = slice(NB * k, NB * k + NB)
                        sp.dma_start(rbf4[slot][rows, :], group_of(A["rbf"], g)).then_inc(s[f"edge{slot}"], 16)
                        sp.dma_start(y16[slot][rows, :], group_of(A["y"], g)[k, :].partition_broadcast(NB)).then_inc(s[f"edge{slot}"], 16)

                def load_dst(g, slot):
                    sp.dma_start(dst_bc[slot][:], group_of(A["dst_rows"], g).partition_broadcast(P)).then_inc(s[f"dst{slot}"], 16)

                def load_more_dst(g, w):
                    wait_apart(sp, s["more_at"], w, s["tick_s"])
                    sp.dma_start(M["dst_more"][:], group_of(A["dst_rows"], g).partition_broadcast(P)).then_inc(s["more_dst"], 16)

                def step(g, slot, use, now, mid, late):
                    if now:
                        if not mid:
                            load_edge(0, 0)
                            load_dst(0, 0)
                        else:
                            wait_apart(sp, s["scaled"], g, s["tick_s"])
                        load_edge(g + 1, 1 - slot)
                        if mid:
                            wait_apart(sp, s["at_node"], g, s["tick_s"])
                        load_dst(g + 1, 1 - slot)
                        if late:
                            wait_apart(sp, s["value_block"], g * 5 - 5, s["tick_s"])
                        y = group_of(A["y"], g)
                        sp.dma_start(y_all[slot][:], y.partition_broadcast(P)).then_inc(s[f"wide{slot}"], 16)
                        for k in range(4):
                            sp.dma_start(y_quad[slot][32 * k:32 * k + 32, :], y[k, :].partition_broadcast(32)).then_inc(s[f"wide{slot}"], 16)
                    window_rows(nc, sp, g, mid, late, window_from, K["least_i"], state, st_in, st_out, s,
                                load_more_dst)

                sp.sem_inc(s["state_out"], 16)
                schedule(step)(sp)
                total = sp.value_load(window_from[0:1, NG:NG + 1], min_val=1, max_val=MAX_W)
                wait_apart(sp, s["state_out"], total * 16 + 16, s["tick_s"])
                sp.wait_ge(s[f"dst{NG % 2}"], 16 * (NG // 2 + 1))

            @block.gpsimd
            def _(pool):
                def wait(sm, value):
                    wait_apart(pool, sm, value, s["tick"])

                def gather(g, slot, use, fresh):
                    if not fresh:
                        wait(s[f"got{slot}"], use * 128)
                    pool.tensor_copy(idx[slot][:], idx_all[:, bass.ds(g, 1), :].rearrange("p a c -> p (a c)")).then_inc(s["indexed"], 1)
                    wait(s["indexed"], g + 1)
                    if not fresh:
                        wait(s["summed"], g - 1)
                    for t in range(TILES):
                        for buf, table, c in ((got_src, src_tab, t), (got_dst, dst_tab, TILES + t)):
                            pool.indirect_dma_start(
                                out=buf[slot][:, t, :], out_offset=None, in_=table[:, :],
                                in_offset=bass.IndirectOffsetOnAxis(ap=idx[slot][:, c:c + 1], axis=0)
                            ).then_inc(s[f"got{slot}"], 16)

                def combine(g, slot, use, fresh):
                    wait(s[f"got{slot}"], use * 128 + 128)
                    if not fresh:
                        wait(s["turned"], g - 1)
                    twice = [P, TILES, 2, CS]
                    pool.tensor_tensor(msg[slot][:, :, 0:2 * CS].rearrange("p t (k c) -> p t k c", k=2),
                                       got_src[slot][:, :, 0:CS].unsqueeze(2).broadcast_to(twice),
                                       got_dst[slot][:, :, 0:CS].unsqueeze(2).broadcast_to(twice), ALU.add)
                    pool.tensor_tensor(msg[slot][:, :, 2 * CS:], got_src[slot][:, :, CS:D], got_dst[slot][:, :, CS:D],
                                       ALU.add).then_inc(s["summed"], 1)
                    wait(s[f"edge{slot}"], use * 128 + 128)
                    if not fresh:
                        wait(s["weighted"], g * 6 - 6)
                    pool.tensor_tensor(edge[slot][:], rbf4[slot][:], y16[slot][:], ALU.mult).then_inc(s["scaled"], 1)

                def step(g, slot, use, now, mid, late):
                    if now:
                        gather(g + 1, 1 - slot, mid_use(slot, use) + 1 if mid else 0, not mid)
                    if late:
                        more_masks(pool, wait, g - 2, K, s, M, slot, A["dst_rows"])
                    if now:
                        wait(s[f"dst{slot}"], use * 16 + 16)
                        first_masks(pool, wait, g, K, s, M, slot, late, dst_bc[slot])
                        combine(g + 1, 1 - slot, mid_use(slot, use) + 1 if mid else 0, not mid)

                pool.sem_inc(s["window_sum"], 1)
                pool.sem_inc(s["more_step"], 1)
                gather(0, 0, 0, True)
                combine(0, 0, 0, True)
                schedule(step)(pool)

            @block.tensor
            def _(pe):
                def spread_logits(p, slot, h):
                    for t in range(TILES):
                        c = t * HEADS + h
                        last = nc.tensor.transpose(ebank(h)[:, P * t:P * t + P],
                                                   logits[slot][:, c:c + 1].broadcast_to([P, P]), ident[:])
                    last.then_inc(s["logit_turned"], 1)

                def top_to_edges(slot):
                    for t in range(TILES):
                        last = nc.tensor.matmul(top_edge[:, HEADS * t:HEADS * t + HEADS], at_node[slot][:, P * t:P * t + P],
                                                top[:], start=True, stop=True)
                    last.then_inc(s["top_at_edge"], 1)

                def sum_window(w, slot):
                    pe.wait_ge(s["merged"], w + 1)
                    pe.wait_ge(s["value_scaled"], w + 1)
                    for t in range(TILES):
                        last = nc.tensor.matmul(win, to_node[slot][:, t, :],
                                                vals[:, HEADS * t:HEADS * t + HEADS, :].rearrange("p h c -> p (h c)"),
                                                start=t == 0, stop=t == TILES - 1)
                    last.then_inc(s["window_sum"], 1)

                def step(g, slot, use, now, mid, late):
                    other = 1 - slot
                    if mid or late:
                        first = first_window(pe, window_from, g - 1)
                    if late:
                        late_first = first_window(pe, window_from, g - 2)
                    if now:
                        pe.wait_ge(s["summed"], g + 1)
                        for t in range(TILES):
                            c = slice(P * t, P * t + P)
                            nc.tensor.transpose(pT[:, c], msg[slot][:, t, 0:2 * CS], ident[:])
                            last = nc.tensor.transpose(pT[0:96, 512 + P * t:640 + P * t], msg[slot][:, t, 2 * CS:], ident[:])
                        last.then_inc(s["turned"], 1)
                    if mid:
                        pe.wait_ge(s["logit"], g)
                        spread_logits(g - 1, other, 0)
                        spread_logits(g - 1, other, 1)
                    if late:
                        sum_window(late_first, slot)

                        def more(w):
                            pe.wait_ge(s["more_masks"], w + 1)
                            pe.wait_ge(s["top"], w + 2)
                            top_to_edges(slot)
                            sum_window(w, slot)
                        more_windows(pe, late_first, first, more)
                    if mid:
                        pe.wait_ge(s["gated"], g)
                        pe.wait_ge(s["scalars"], g)
                        if now:
                            pe.wait_ge(s["turned_copied"], g + 1)
                        for t in range(TILES):
                            nc.tensor.transpose(pT[:, P * t:P * t + P], gated[other][:, t, 0:P], ident[:])
                            last = nc.tensor.transpose(pT[:, 512 + P * t:640 + P * t], gated[other][:, t, P:2 * P], ident[:])
                        last.then_inc(s["value_turned"], 1)
                        for h in (2, 3):
                            pe.wait_ge(s["logit_copied"], g * 4 - 4 + h - 1)
                            spread_logits(g - 1, other, h)
                    if now:
                        def weigh(b):
                            m = P if b < 2 else 96
                            if b == 0:
                                pe.wait_ge(s["scaled"], g + 1)
                            if b < 2 and mid:
                                pe.wait_ge(s["logit_copied"], g * 4 - 1 + b)
                            if b >= 2:
                                pe.wait_ge(s["block_done"], g * 6 + b - 1)
                            nc.tensor.matmul(ebank(b)[0:m, :], w_edge[:, b, 0:m], edge[slot][:], start=True,
                                             stop=True).then_inc(s["weighted"], 1)

                        def add_block(t, b):
                            c0, c1 = ((0, 256), (32, 96), (96, 256), (0, 96), (0, 96), (0, 96))[b]
                            m = P if b < 2 else 96
                            return nc.tensor.matmul(messages[:, t, c0:c1], blocks[0:m, b, P * t:P * t + P],
                                                    w_msg[0:m, b, c0:c1], start=b == 0, stop=b == 5)

                        weigh(0)
                        weigh(1)
                        for b in range(6):
                            if b < 4:
                                weigh(b + 2)
                            pe.wait_ge(s["block_done"], g * 6 + b + 1)
                            for t in (0, 2):
                                add_block(t, b)
                        for t in (1, 3):
                            for b in range(6):
                                last = add_block(t, b)
                        last.then_inc(s["message"], 1)
                    if mid:
                        pe.wait_ge(s["first_masks"], g)
                        pe.wait_ge(s["top"], first + 2)
                        top_to_edges(other)
                        pe.wait_ge(s["value_block"], g * 5)
                        for t in range(TILES):
                            if t == 2:
                                pe.wait_ge(s["top_read"], first + 1)
                            for b in range(5):
                                last = nc.tensor.matmul(value_tile(t), vblocks[:, b, P * t:P * t + P], w_val[:, b, :],
                                                        start=b == 0, stop=b == 4)
                        last.then_inc(s["value"], 1)
                schedule(step)(pe)

            @block.scalar
            def _(act):
                def make_far(w, slot):
                    act.wait_ge(s["top"], w + 1)
                    nc.scalar.activation(far[:], at_node[slot][:], ACT.Copy, scale=-LEAST, bias=LEAST).then_inc(s["far"], 1)

                def exponentials(w):
                    act.wait_ge(s["window_sum"], w + 1)
                    act.wait_ge(s["shifted"], w + 1)
                    nc.scalar.activation(vals[:, :, 0], shift[:], ACT.Exp).then_inc(s["expd"], 1)
                    act.wait_ge(s["rescale"], w + 1)
                    nc.scalar.activation(fac[:], diff[:], ACT.Exp).then_inc(s["factors"], 1)

                def step(g, slot, use, now, mid, late):
                    other = 1 - slot
                    if now:
                        act.wait_ge(s["turned"], g + 1)
                        if mid:
                            act.wait_ge(s["block_done"], g * 6)
                        nc.scalar.activation(sT2[:], pT[:, 0:512], ACT.Copy)
                        nc.scalar.activation(vT[:], pT[0:96, 512:1024], ACT.Copy).then_inc(s["turned_copied"], 1)
                    if mid:
                        for h in range(HEADS):
                            act.wait_ge(s["logit_turned"], g * 4 - 4 + h + 1)
                            nc.scalar.activation(logit_bc[other][:, h, :], ebank(h), ACT.Copy).then_inc(s["logit_copied"], 1)
                    if late:
                        first = first_window(act, window_from, g - 2)
                        end = first_window(act, window_from, g - 1)

                        def more(w):
                            act.wait_ge(s["more_at"], w + 1)
                            make_far(w, slot)
                            exponentials(w)
                        more_windows(act, first, end, more)
                    if mid:
                        first = first_window(act, window_from, g - 1)
                        act.wait_ge(s["at_node"], g)
                        make_far(first, other)
                    if now:
                        act.wait_ge(s["message"], g + 1)
                        nc.scalar.activation(th[:], messages[:, :, 96:192], ACT.Tanh, scale=0.5).then_inc(s["tanh"], 1)
                        nc.scalar.activation(rl[:], messages[:, :, 192:256], ACT.Relu, scale=0.8).then_inc(s["relu"], 1)
                        act.wait_ge(s["tanh"], g + 1)
                        nc.scalar.activation(gated[slot][:, :, 96:128], th[:, :, 0:32], ACT.Copy, bias=1.0)
                        nc.scalar.activation(gated[slot][:, :, 128:256].rearrange("p t (k c) -> p t k c", k=4),
                                             th[:, :, 32:64].unsqueeze(2).broadcast_to([P, TILES, 4, 32]),
                                             ACT.Copy, bias=1.0).then_inc(s["scalars"], 1)
                    if mid:
                        exponentials(first)
                schedule(step)(act)

            @block.vector
            def _(dve):
                def take_top(w, slot):
                    dve.wait_ge(s["far"], w + 1)
                    dve.sem_inc(s["tick_v"], 1)
                    for h in range(HEADS):
                        last = dve.tensor_tensor_reduce(out=junk[:, h, :], in0=logit_bc[slot][:, h, :], in1=far[:], scale=1.0,
                                                        scalar=LEAST, op0=ALU.add, op1=ALU.max, accum_out=top[:, h:h + 1])
                    last.then_inc(s["top"], 1)

                def shift_logits(w, slot):
                    dve.wait_ge(s["top_at_edge"], w + 1)
                    dve.tensor_tensor(shift[:], logits[slot][:], top_edge, ALU.subtract).then_inc(s["top_read"], 1)
                    dve.wait_ge(s["top_read"], w + 1)
                    dve.tensor_scalar(shift[:], shift[:], 1.0, None, ALU.min).then_inc(s["shifted"], 1)
                    dve.wait_ge(s["state_in"], w * 16 + 16)
                    dve.tensor_tensor(st_out[:, 0:HEADS], st_in[:, 0:HEADS], top[:], ALU.max).then_inc(s["win_step"], 1)
                    dve.wait_ge(s["win_step"], w * 2 + 1)
                    dve.tensor_tensor(diff[:, 0:HEADS], st_in[:, 0:HEADS], st_out[:, 0:HEADS], ALU.subtract)
                    dve.tensor_tensor(diff[:, HEADS:2 * HEADS], top[:], st_out[:, 0:HEADS], ALU.subtract).then_inc(s["rescale"], 1)

                def scale_values(w):
                    dve.wait_ge(s["expd"], w + 1)
                    dve.tensor_tensor(vals[:, :, 1:HW].rearrange("p (b h) c -> p b h c", b=2),
                                      pV[:].rearrange("p (b c) -> p b c", b=2)[:, :, 0:320].rearrange("p b (h c) -> p b h c", c=HW - 1),
                                      vals[:, :, 0:1].rearrange("p (b h) c -> p b h c", b=2).broadcast_to([P, 2, 2 * HEADS, HW - 1]),
                                      ALU.mult).then_inc(s["value_scaled"], 1)

                def merge(w):
                    dve.wait_ge(s["factors"], w + 1)
                    dve.tensor_tensor(heads(part[:, 0, :]), heads(st_in[:, HEADS:SW]),
                                      fac[:, 0:HEADS].unsqueeze(2).broadcast_to([P, HEADS, HW]), ALU.mult)
                    dve.wait_ge(s["window_sum"], w + 2)
                    dve.tensor_tensor(heads(part[:, 1, :]), heads(win),
                                      fac[:, HEADS:2 * HEADS].unsqueeze(2).broadcast_to([P, HEADS, HW]), ALU.mult).then_inc(s["win_step"], 1)
                    dve.wait_ge(s["win_step"], w * 2 + 2)
                    dve.tensor_tensor(st_out[:, HEADS:SW], part[:, 0, :], part[:, 1, :], ALU.add).then_inc(s["merged"], 1)

                def step(g, slot, use, now, mid, late):
                    other = 1 - slot
                    if late:
                        first = first_window(dve, window_from, g - 2)
                        end = first_window(dve, window_from, g - 1)
                        merge(first)

                        def more(w):
                            take_top(w, slot)
                            shift_logits(w, slot)
                            scale_values(w)
                            merge(w)
                        more_windows(dve, first, end, more)
                    def make_value_block(k):
                        if k < 4:
                            dve.tensor_tensor(vblocks[:, k, :], pT[:, 0:512], y_all[other][:, k, :], ALU.mult).then_inc(s["value_block"], 1)
                        else:
                            dve.tensor_tensor(vblocks[:, 4, :], pT[:, 512:1024], y_quad[other][:], ALU.mult).then_inc(s["value_block"], 1)

                    if mid:
                        dve.wait_ge(s[f"wide{other}"], mid_use(slot, use) * 80 + 80)
                        dve.wait_ge(s["value_turned"], g)
                        for k in range(4):
                            make_value_block(k)
                        if not now:
                            make_value_block(4)
                    if now:
                        for b in range(6):
                            if b == 2 and mid:
                                make_value_block(4)
                            m = P if b < 2 else 96
                            dve.wait_ge(s["weighted"], g * 6 + b + 1)
                            if b == 0:
                                dve.wait_ge(s["turned_copied"], g + 1)
                            dve.tensor_tensor(blocks[0:m, b, :], ebank(b)[0:m, :], (sT2 if b < 2 else vT)[0:m, :],
                                              ALU.mult).then_inc(s["block_done"], 1)
                    if mid:
                        first = first_window(dve, window_from, g - 1)
                        dve.wait_ge(s["logit_copied"], g * 4)
                        dve.sem_inc(s["tick_v"], 1)
                        take_top(first, other)
                        shift_logits(first, other)
                    if now:
                        dve.wait_ge(s["tanh"], g + 1)
                        dve.tensor_scalar(gates[:], th[:, :, 64:96], 1.0, None, ALU.add).then_inc(s["gate"], 1)
                        dve.wait_ge(s["gate"], g + 1)
                        dve.wait_ge(s["relu"], g + 1)
                        dve.tensor_tensor(gated[slot][:, :, 0:96].rearrange("p t (x d) -> p t x d", x=3),
                                          messages[:, :, 0:96].rearrange("p t (x d) -> p t x d", x=3),
                                          gates[:].unsqueeze(2).broadcast_to([P, TILES, 3, CV]),
                                          ALU.mult).then_inc(s["gated"], 1)
                        dve.scalar_tensor_tensor(lg[:], messages[:, :, 192:256], 0.2, rl[:], ALU.mult, ALU.add).then_inc(s["logit_step"], 1)
                        dve.wait_ge(s["logit_step"], g * 2 + 1)
                        dve.tensor_tensor(lg[:], lg[:], adot[:].unsqueeze(1).broadcast_to([P, TILES, 64]), ALU.mult).then_inc(s["logit_step"], 1)
                        dve.wait_ge(s["logit_step"], g * 2 + 2)
                        dve.tensor_reduce(logits[slot][:], lg[:].rearrange("p t (h c) -> p (t h) c", h=HEADS), axis=AX.X,
                                          op=ALU.add).then_inc(s["logit"], 1)
                    if mid:
                        dve.wait_ge(s["value"], g)
                        scale_values(first)
                dve.sem_inc(s["merged"], 1)
                dve.sem_inc(s["top"], 1)
                schedule(step)(dve)


def window_rows(nc, sp, g, mid, late, window_from, least_i, table, st_in, st_out, s, load_more_dst=None):
    def row_of(q, steps):
        at = slice(q, q + 1) if isinstance(q, int) else bass.ds(q, 1)
        least = sp.value_load(least_i[0:1, at], min_val=0, max_val=N_NODES)
        return nc.s_assert_within(least + steps * P, 0, STATE_ROWS - P)

    def load(w, row):
        wait_apart(sp, s["state_out"], w * 16 + 16, s["tick_s"])
        sp.dma_start(st_in[:], table[bass.ds(row, P), :]).then_inc(s["state_in"], 16)

    def store(w, row):
        wait_apart(sp, s["merged"], w + 2, s["tick_s"])
        sp.dma_start(table[bass.ds(row, P), :], st_out[:]).then_inc(s["state_out"], 16)

    if late:
        first = first_window(sp, window_from, g - 2)
        end = first_window(sp, window_from, g - 1)
        store(first, row_of(g - 2, 0))
        if load_more_dst is not None:
            sp.sem_inc(s["more_dst"], 16)

        def more(w):
            row = row_of(g - 2, w - first)
            if load_more_dst is not None:
                load_more_dst(g - 2, w)
            load(w, row)
            store(w, row)
        more_windows(sp, first, end, more)
    if mid:
        load(first_window(sp, window_from, g - 1), row_of(g - 1, 0))


def relate(pool, wait, g, K, s, M):
    at = slice(g, g + 1) if isinstance(g, int) else bass.ds(g, 1)
    least = K["least_bc"][:, at]
    pool.tensor_tensor(M["rel"][:], M["dst_f"][:], least.broadcast_to([P, TILES]), ALU.subtract)
    pool.tensor_tensor(M["first_node"][:], K["iota_col"][:], least, ALU.add).then_inc(s["related"], 1)


def masks(pool, M, slot, dst_bc, done_at, done):
    if dst_bc is not None:
        pool.tensor_scalar(M["at_node"][slot][:], dst_bc[:], M["first_node"][:, 0:1], None, ALU.is_equal).then_inc(done_at, 1)
    for t in range(TILES):
        last = pool.tensor_scalar(M["to_node"][slot][:, t, :], M["iota_row"][:], M["rel"][:, t:t + 1], None, ALU.is_equal)
    last.then_inc(done, 1)


def first_masks(pool, wait, g, K, s, M, slot, late, dst_bc):
    at = slice(g, g + 1) if isinstance(g, int) else bass.ds(g, 1)
    if late:
        wait(s["window_sum"], first_window(pool, K["window_from"], g - 1) + 1)
    pool.tensor_copy(M["dst_f"][:], K["idx_all"][:, at, TILES:2 * TILES].rearrange("p a c -> p (a c)")).then_inc(s["dst_taken"], 1)
    wait(s["dst_taken"], g + 1)
    relate(pool, wait, g, K, s, M)
    wait(s["related"], g + 1)
    masks(pool, M, slot, dst_bc, s.get("at_node"), s["first_masks"])
    wait(s["first_masks"], g + 1)


def more_masks(pool, wait, g, K, s, M, slot, dst_rows):
    at = slice(g, g + 1) if isinstance(g, int) else bass.ds(g, 1)
    first = first_window(pool, K["window_from"], g)
    end = first_window(pool, K["window_from"], g + 1)

    def more(w):
        wait(s["window_sum"], w + 1)
        if dst_rows is not None:
            wait(s["more_dst"], w * 16 + 16)
        pool.tensor_copy(M["dst_f"][:], K["idx_all"][:, at, TILES:2 * TILES].rearrange("p a c -> p (a c)")).then_inc(s["more_step"], 1)
        wait(s["more_step"], w * 4 + 2)
        least = K["least_bc"][:, at]
        pool.tensor_tensor(M["rel"][:], M["dst_f"][:], least.broadcast_to([P, TILES]), ALU.subtract)
        pool.tensor_tensor(M["first_node"][:], K["iota_col"][:], least, ALU.add).then_inc(s["more_step"], 1)
        wait(s["more_step"], w * 4 + 3)
        pool.tensor_tensor(M["rel"][:], M["rel"][:], M["down"][:].broadcast_to([P, TILES]), ALU.subtract)
        pool.tensor_tensor(M["first_node"][:], M["first_node"][:], M["down"][:], ALU.add).then_inc(s["more_step"], 1)
        wait(s["more_step"], w * 4 + 4)
        masks(pool, M, slot, None if dst_rows is None else M["dst_more"], s.get("more_at"), s["more_masks"])
        pool.tensor_scalar(M["down"][:], M["down"][:], float(P), None, ALU.add).then_inc(s["more_step"], 1)
        wait(s["more_step"], w * 4 + 5)
        wait(s["more_masks"], w + 1)

    wait(s["more_step"], first * 4 + 1)
    pool.memset(M["down"][:], float(P)).then_inc(s["more_step"], 4)
    pool.sem_inc(s["more_masks"], 1)
    if dst_rows is not None:
        pool.sem_inc(s["more_at"], 1)
    with pool.If(first + 1 < end):
        with pool.Fori(first + 1, end) as w:
            more(w)


def node1(nc, ctx, A, K):
    keep, ident, psum, state, attr = (K[n] for n in ("keep", "ident", "psum", "state", "attr"))
    chunk_rows, normalize, project_pe, project_act = (K[n] for n in ("chunk_rows", "normalize", "project_pe", "project_act"))
    with ExitStack() as sx:
        def tmp(name, shape, dt=F32):
            return sx.enter_context(nc.sbuf_tensor(name, shape, dt))
        st = tmp("st", [P, CH, SW])
        agg = tmp("agg", [P, CH, D])
        den = tmp("den", [P, 2, CH, HEADS])
        agg_ta = tmp("agg_ta", [P, CH * P])
        agg_tb = tmp("agg_tb", [CV, CH * P])
        res = tmp("res", [P, CH, D])
        x1 = tmp("x1", [P, CH, D])
        cen = tmp("cen1", [P, CH, D])
        sq = tmp("sq1", [P, CH, D])
        node = tmp("node1", [P, CH, D])
        both = tmp("both1", [P, 2, CH, D])
        f_out = tmp("f_out", [P, CH, CS + D])
        stats = tmp("stats1", [P, 3, CH])
        S = {n: ctx.enter_context(nc.semaphore("n1_" + n)) for n in (
            "x", "var", "std", "node", "tr", "trc", "pj", "pjc", "ch", "tick", "out", "agg", "at", "atc", "res", "resc", "f")}
        S["nts"] = tmp("nts1", [64, CH * P])
        S["ntv"] = tmp("ntv1", [96, CH * P])

        with nc.Block() as block:
            @block.sync
            def _(sp):
                with sp.Fori(0, NCH) as it:
                    sp.dma_start(st[:], chunk_rows(state[0:NODES_PAD, :], it)).then_inc(S["x"], 16)
                    sp.wait_ge(S["f"], it + 1)
                    sp.dma_start(chunk_rows(K["f_tab"], it), f_out[:]).then_inc(S["out"], 16)
                    wait_apart(sp, S["out"], it * 16 + 16, S["tick"])

            @block.vector
            def _(dve):
                chain = Chain(dve, S["ch"], 14)
                with dve.Fori(0, NCH) as it:
                    chain.begin(it)
                    mine = bass.ds(it * CH, CH)
                    dve.wait_ge(S["x"], it * 16 + 16)
                    by_head = st[:, :, HEADS:SW].rearrange("p t (h c) -> p t h c", h=HEADS)
                    chain.step(dve.tensor_scalar(den[:, 0, :, :], by_head[:, :, :, 0], 1e-16, None, ALU.add))
                    chain.step(dve.reciprocal(den[:, 1, :, :], den[:, 0, :, :]))
                    dve.tensor_tensor(agg[:].rearrange("p t (h c) -> p t h c", h=HEADS), by_head[:, :, :, 1:HW],
                                      den[:, 1, :, :].unsqueeze(3).broadcast_to([P, CH, HEADS, HW - 1]), ALU.mult).then_inc(S["agg"], 1)
                    dve.wait_ge(S["resc"], it * CH + CH)
                    chain.step(dve.tensor_tensor(x1[:, :, 0:CS], res[:, :, 0:CS], keep[:, mine, 0:CS], ALU.add))
                    for x in range(3):
                        last = dve.tensor_tensor(x1[:, :, CS + x:D:3], res[:, :, CS + CV * x:CS + CV * x + CV],
                                                 keep[:, mine, CS + x:D:3], ALU.add)
                    chain.step(last)
                    normalize(dve, chain, x1[:], (cen[:], sq[:]), stats, S["var"], S["std"], it + 1)
                    chain.step(dve.tensor_tensor(cen[:], cen[:], stats[:, 2, :].unsqueeze(2).broadcast_to([P, CH, D]), ALU.mult))
                    dve.tensor_scalar(node[:, :, 0:CS], cen[:, :, 0:CS], 0.0, None, ALU.max)
                    for x in range(3):
                        last = dve.tensor_scalar(node[:, :, CS + CV * x:CS + CV * x + CV], cen[:, :, CS + x:D:3], 0.0, None, ALU.max)
                    last.then_inc(S["node"], 1)
                    dve.wait_ge(S["pjc"], it * CH + CH)
                    by_attr = attr[:, mine].unsqueeze(2).broadcast_to([P, CH, D])
                    for c in (0, CS):
                        dve.tensor_tensor(f_out[:, :, c:c + CS], both[:, 0, :, 0:CS], by_attr[:, :, 0:CS], ALU.mult)
                    dve.tensor_tensor(f_out[:, :, 2 * CS:], both[:, 0, :, CS:D], by_attr[:, :, CS:D], ALU.mult).then_inc(S["f"], 1)
                    chain.step(dve.tensor_tensor(res[:], both[:, 1, :, :], by_attr, ALU.mult))
                    chain.step(dve.tensor_tensor(keep[:, mine, 0:CS], res[:, :, 0:CS], x1[:, :, 0:CS], ALU.add))
                    for x in range(3):
                        last = dve.tensor_tensor(keep[:, mine, CS + x:D:3], res[:, :, CS + CV * x:CS + CV * x + CV],
                                                 x1[:, :, CS + x:D:3], ALU.add)
                    chain.step(last)
                    chain.end()

            @block.scalar
            def _(act):
                with act.Fori(0, NCH) as it:
                    act.wait_ge(S["at"], it + 1)
                    nc.scalar.activation(agg_ta[:], psum[0][:, 0:CH * P], ACT.Copy)
                    nc.scalar.activation(agg_tb[:], psum[1][0:CV, 0:CH * P], ACT.Copy).then_inc(S["atc"], 1)
                    for t in range(CH):
                        act.wait_ge(S["res"], it * CH + t + 1)
                        nc.scalar.activation(res[:, t, :], psum[2 + t % 2][:, 0:D], ACT.Copy).then_inc(S["resc"], 1)
                    act.wait_ge(S["var"], it + 1)
                    nc.scalar.activation(stats[:, 1, :], stats[:, 1, :], ACT.Sqrt).then_inc(S["std"], 1)
                    project_act(act, it, both, S)

            @block.tensor
            def _(pe):
                with pe.Fori(0, NCH) as it:
                    pe.wait_ge(S["agg"], it + 1)
                    for t in range(CH):
                        c = slice(t * P, (t + 1) * P)
                        nc.tensor.transpose(psum[0][:, c], agg[:, t, 0:P], ident[:])
                        last = nc.tensor.transpose(psum[1][0:CV, c], agg[:, t, P:D], ident[:])
                    last.then_inc(S["at"], 1)
                    pe.wait_ge(S["atc"], it + 1)
                    for t in range(CH):
                        c = slice(t * P, (t + 1) * P)
                        if t >= 2:
                            pe.wait_ge(S["resc"], it * CH + t - 1)
                        nc.tensor.matmul(psum[2 + t % 2][:, 0:D], agg_ta[:, c], K["w_out_a"][:], start=True, stop=False)
                        nc.tensor.matmul(psum[2 + t % 2][:, 0:D], agg_tb[:, c], K["w_out_b"][:], start=False,
                                         stop=True).then_inc(S["res"], 1)
                    project_pe(pe, it, node, K["w_n1s"], K["w_n1v"], S)


def layer1(nc, ctx, A, K):
    ident, idx_all, window_from, psum, sums, f_tab = (K[n] for n in ("ident", "idx_all", "window_from", "psum", "sums", "f_tab"))
    s = {n: ctx.enter_context(nc.semaphore("l1_" + n)) for n in (
        "edge0", "edge1", "wide0", "wide1", "got0", "got1", "indexed", "hidden_raw", "hid_tanh", "hidden", "turned",
        "turned_copied", "weight", "product", "scaled_product", "edge_sums", "scal_copied", "vec_step", "edge_value",
        "window_sum", "merged", "state_in", "state_out", "tick", "tick_s", "ones", "first_masks",
        "dst_taken", "related", "more_masks", "more_step")}
    with ExitStack() as sx:
        def tmp(name, shape, dt=F32):
            return sx.enter_context(nc.sbuf_tensor(name, shape, dt))
        idx = [tmp(f"idx1{i}", [P, TILES], I32) for i in range(2)]
        got = [tmp(f"gotf{i}", [P, TILES, CS + D]) for i in range(2)]
        rbf = [tmp(f"rbf{i}", [NB, GE]) for i in range(2)]
        y_scal = [tmp(f"y_scal{i}", [P, GE]) for i in range(2)]
        y_vec = [tmp(f"y_vec{i}", [96, GE]) for i in range(2)]
        y_edge = [tmp(f"y_edge{i}", [P, TILES, 4]) for i in range(2)]
        th = tmp("th1", [64, GE])
        hid = [tmp(f"hid{i}", [64, GE]) for i in range(2)]
        e0T = [tmp(f"e0T{i}", [P, GE]) for i in range(2)]
        e1T = [tmp(f"e1T{i}", [96, GE]) for i in range(2)]
        prod = tmp("prod", [P, 3, GE])
        val = [tmp(f"val{i}", [P, TILES, QW]) for i in range(2)]
        vec = tmp("vec", [P, 2, TILES, 96])
        to_node = [tmp(f"to_node1{i}", [P, TILES, P]) for i in range(2)]
        M = {"to_node": to_node, "iota_row": K["iota_row"], "dst_f": tmp("dst_f1", [P, TILES]),
             "rel": tmp("rel1", [P, TILES]), "first_node": tmp("first_node1", [P, 1]), "down": tmp("down1", [P, 1])}
        st_in = tmp("st_in1", [P, QW])
        st_out = tmp("st_out1", [P, QW])
        pT, pW, pE, pS = psum
        win, raw = pS[:, 0:QW], pS[0:64, 512:1024]

        def edge_tile(t, c0, c1):
            o = 512 * (t // 2) + 193 * (t % 2)
            return pE[:, o + c0:o + c1]

        by_tile = pE[:].rearrange("p (b c) -> p b c", b=2)[:, :, 0:386].rearrange("p b (t c) -> p b t c", t=2)

        with nc.Block() as block:
            @block.sync
            def _(sp):
                def load_rbf(g, slot):
                    sp.dma_start(rbf[slot][:], group_of(A["rbf"], g)).then_inc(s[f"edge{slot}"], 16)

                def step(g, slot, use, now, mid, late):
                    if now:
                        if not mid:
                            load_rbf(0, 0)
                        else:
                            wait_apart(sp, s["hidden_raw"], g, s["tick_s"])
                        load_rbf(g + 1, 1 - slot)
                        if late:
                            wait_apart(sp, s["edge_value"], g - 1, s["tick_s"])
                        e, y = s[f"wide{slot}"], group_of(A["y"], g)
                        sp.dma_start(y_scal[slot][0:64, :], y[0, :].partition_broadcast(64)).then_inc(e, 16)
                        for x in range(3):
                            sp.dma_start(y_vec[slot][32 * x:32 * x + 32, :], y[x + 1, :].partition_broadcast(32)).then_inc(e, 16)
                        sp.dma_start(y_edge[slot][:], group_of(A["y_edge"], g)).then_inc(e, 16)
                    window_rows(nc, sp, g, mid, late, window_from, K["least_i"], sums, st_in, st_out, s)

                sp.sem_inc(s["state_out"], 16)
                schedule(step)(sp)
                total = sp.value_load(window_from[0:1, NG:NG + 1], min_val=1, max_val=MAX_W)
                wait_apart(sp, s["state_out"], total * 16 + 16, s["tick_s"])
                sp.wait_ge(s[f"edge{NG % 2}"], 16 * (NG // 2 + 1))

            @block.gpsimd
            def _(pool):
                def wait(sm, value):
                    wait_apart(pool, sm, value, s["tick"])

                def gather(g, slot, use, fresh):
                    if not fresh:
                        wait(s[f"got{slot}"], use * 64)
                    pool.tensor_copy(idx[slot][:], idx_all[:, bass.ds(g, 1), 0:TILES].rearrange("p a c -> p (a c)")).then_inc(s["indexed"], 1)
                    wait(s["indexed"], g + 1)
                    if not fresh:
                        wait(s["turned"], g - 1)
                    for t in range(TILES):
                        pool.indirect_dma_start(
                            out=got[slot][:, t, :], out_offset=None, in_=f_tab[:, :],
                            in_offset=bass.IndirectOffsetOnAxis(ap=idx[slot][:, t:t + 1], axis=0)
                        ).then_inc(s[f"got{slot}"], 16)

                def step(g, slot, use, now, mid, late):
                    if now:
                        gather(g + 1, 1 - slot, mid_use(slot, use) + 1 if mid else 0, not mid)
                    if late:
                        more_masks(pool, wait, g - 2, K, s, M, slot, None)
                    if mid:
                        first_masks(pool, wait, g - 1, K, s, M, 1 - slot, late, None)

                pool.sem_inc(s["window_sum"], 1)
                pool.sem_inc(s["more_step"], 1)
                gather(0, 0, 0, True)
                schedule(step)(pool)
                pool.wait_ge(s[f"got{NG % 2}"], 64 * (NG // 2 + 1))

            @block.tensor
            def _(pe):
                def sum_window(w, slot):
                    pe.wait_ge(s["merged"], w + 1)
                    for t in range(TILES):
                        last = nc.tensor.matmul(win, to_node[slot][:, t, :], val[slot][:, t, :], start=t == 0,
                                                stop=t == TILES - 1)
                    last.then_inc(s["window_sum"], 1)

                def step(g, slot, use, now, mid, late):
                    other = 1 - slot
                    if late:
                        first = first_window(pe, window_from, g - 2)
                        end = first_window(pe, window_from, g - 1)
                    if mid:
                        pe.wait_ge(s["hidden"], g)
                        nc.tensor.matmul(pW[:, 512:1024], K["w_f01"][:], hid[other][:], start=True, stop=True).then_inc(s["weight"], 1)
                    if now:
                        pe.wait_ge(s[f"edge{slot}"], use * 16 + 16)
                        nc.tensor.matmul(raw, K["w_fc1"][:], rbf[slot][:], start=True, stop=True).then_inc(s["hidden_raw"], 1)
                        pe.wait_ge(s[f"got{slot}"], use * 64 + 64)
                        if mid:
                            pe.wait_ge(s["turned_copied"], g)
                        for t in range(TILES):
                            nc.tensor.transpose(pT[:, P * t:P * t + P], got[slot][:, t, 0:2 * CS], ident[:])
                            last = nc.tensor.transpose(pT[0:96, 512 + P * t:640 + P * t], got[slot][:, t, 2 * CS:], ident[:])
                        last.then_inc(s["turned"], 1)
                    if mid:
                        nc.tensor.matmul(pW[0:96, 0:512], K["w_f3"][:], hid[other][:], start=True, stop=True).then_inc(s["weight"], 1)
                        pe.wait_ge(s["product"], g * 3 - 2)
                        nc.tensor.matmul(pW[0:96, 512:1024], K["w_f2"][:], hid[other][:], start=True, stop=True).then_inc(s["weight"], 1)
                    if late:
                        pe.wait_ge(s["first_masks"], g - 1)
                        pe.wait_ge(s["edge_value"], g - 1)
                        sum_window(first, slot)

                        def more(w):
                            pe.wait_ge(s["more_masks"], w + 1)
                            sum_window(w, slot)
                        more_windows(pe, first, end, more)
                    if mid:
                        pe.wait_ge(s["product"], g * 3)
                        pe.wait_ge(s["scaled_product"], g * 2)
                        for t in range(TILES):
                            c = slice(P * t, P * t + P)
                            nc.tensor.matmul(edge_tile(t, 0, 97), prod[:, 0, c], K["w_c1"][:], start=True, stop=False)
                            nc.tensor.matmul(edge_tile(t, 0, 65), prod[0:96, 1, c], K["w_c2"][:], start=False, stop=False)
                            last = nc.tensor.matmul(edge_tile(t, 97, 193), prod[0:96, 2, c], K["w_c3"][:], start=False, stop=True)
                        last.then_inc(s["edge_sums"], 1)
                schedule(step)(pe)

            @block.scalar
            def _(act):
                def step(g, slot, use, now, mid, late):
                    other = 1 - slot
                    if now:
                        act.wait_ge(s["hidden_raw"], g + 1)
                        nc.scalar.activation(th[:], raw, ACT.Tanh, scale=0.125).then_inc(s["hid_tanh"], 1)
                        act.wait_ge(s["turned"], g + 1)
                        nc.scalar.activation(e0T[slot][:], pT[:, 0:512], ACT.Copy)
                        nc.scalar.activation(e1T[slot][:], pT[0:96, 512:1024], ACT.Copy).then_inc(s["turned_copied"], 1)
                    if mid:
                        act.wait_ge(s["edge_sums"], g)
                        if not late:
                            act.wait_ge(s["ones"], 2)
                        nc.scalar.activation(val[other][:, :, 0:65].rearrange("p (b t) c -> p b t c", b=2), by_tile[:, :, :, 0:65],
                                             ACT.Copy).then_inc(s["scal_copied"], 1)
                schedule(step)(act)

            @block.vector
            def _(dve):
                def merge(w):
                    dve.wait_ge(s["state_in"], w * 16 + 16)
                    dve.wait_ge(s["window_sum"], w + 2)
                    dve.tensor_tensor(st_out[:], st_in[:], win, ALU.add).then_inc(s["merged"], 1)

                def step(g, slot, use, now, mid, late):
                    other = 1 - slot
                    if mid:
                        dve.wait_ge(s["turned_copied"], g)
                        dve.wait_ge(s["weight"], g * 3 - 2)
                        dve.tensor_tensor(prod[:, 0, :], pW[:, 512:1024], e0T[other][:], ALU.mult).then_inc(s["product"], 1)
                    if now:
                        dve.wait_ge(s["hid_tanh"], g + 1)
                        dve.scalar_tensor_tensor(hid[slot][:], th[:], 1.0, raw, ALU.add, ALU.mult).then_inc(s["hidden"], 1)
                    if mid:
                        dve.wait_ge(s["weight"], g * 3 - 1)
                        dve.tensor_tensor(prod[0:96, 1, :], pW[0:96, 0:512], e1T[other][:], ALU.mult).then_inc(s["product"], 1)
                        dve.wait_ge(s[f"wide{other}"], mid_use(slot, use) * 80 + 80)
                        dve.wait_ge(s["product"], g * 3 - 2)
                        dve.tensor_tensor(prod[:, 0, :], prod[:, 0, :], y_scal[other][:], ALU.mult).then_inc(s["scaled_product"], 1)
                        dve.wait_ge(s["weight"], g * 3)
                        dve.tensor_tensor(prod[0:96, 2, :], pW[0:96, 512:1024], e1T[other][:], ALU.mult).then_inc(s["product"], 1)
                        dve.wait_ge(s["product"], g * 3 - 1)
                        dve.tensor_tensor(prod[0:96, 1, :], prod[0:96, 1, :], y_vec[other][:], ALU.mult).then_inc(s["scaled_product"], 1)
                    if late:
                        first = first_window(dve, window_from, g - 2)
                        end = first_window(dve, window_from, g - 1)
                        merge(first)
                        more_windows(dve, first, end, merge)
                    if mid:
                        dve.wait_ge(s["edge_sums"], g)
                        dve.wait_ge(s["scal_copied"], g)
                        for t in range(0, TILES, 2):
                            o = by_tile[:, t // 2, :, :]
                            y = y_edge[other][:, t:t + 2, :]
                            dve.tensor_tensor(vec[:, 0, t:t + 2, :], o[:, :, 97:193], y[:, :, 0:1].broadcast_to([P, 2, 96]), ALU.mult)
                            last = dve.tensor_tensor(vec[:, 1, t:t + 2, :].rearrange("p t (x d) -> p t x d", x=3),
                                                     o[:, :, 65:97].unsqueeze(2).broadcast_to([P, 2, 3, CV]),
                                                     y[:, :, 1:4].unsqueeze(3).broadcast_to([P, 2, 3, CV]), ALU.mult)
                        last.then_inc(s["vec_step"], 1)
                        dve.wait_ge(s["vec_step"], g)
                        dve.tensor_tensor(val[other][:, :, 65:161], vec[:, 0, :, :], vec[:, 1, :, :], ALU.add).then_inc(s["edge_value"], 1)
                for i in range(2):
                    dve.memset(y_scal[i][64:128, :], 1.0)
                    dve.memset(val[i][:, :, QW - 1:QW], 1.0).then_inc(s["ones"], 1)
                dve.wait_ge(s["ones"], 2)
                dve.sem_inc(s["merged"], 1)
                schedule(step)(dve)


def node2(nc, ctx, A, K, out):
    keep, sums, attr, chunk_rows = (K[n] for n in ("keep", "sums", "attr", "chunk_rows"))
    with ExitStack() as sx:
        def tmp(name, shape, dt=F32):
            return sx.enter_context(nc.sbuf_tensor(name, shape, dt))
        S = {n: ctx.enter_context(nc.semaphore("n2_" + n)) for n in ("x0", "x1", "ch", "res", "out0", "out1")}
        q = [tmp(f"q{i}", [P, CH, QW]) for i in range(2)]
        r = [tmp(f"r{i}", [P, CH, D]) for i in range(2)]
        f = tmp("f", [P, 4, CH])
        out_rows = out.rearrange("(c t p) f -> c p t f", t=CH, p=P)
        sum_rows = sums[0:NODES_PAD, :].rearrange("(c t p) f -> c p t f", t=CH, p=P)
        with nc.Block() as block:
            @block.sync
            def _(sp):
                for c in range(NCH):
                    if c >= 2:
                        sp.wait_ge(S["res"], c - 1)
                    sp.dma_start(q[c % 2][:], sum_rows[c]).then_inc(S[f"x{c % 2}"], 16)
                    if c >= 1:
                        sp.wait_ge(S["res"], c)
                        sp.dma_start(out_rows[c - 1], r[(c - 1) % 2][:]).then_inc(S[f"out{(c - 1) % 2}"], 16)
                sp.wait_ge(S["res"], NCH)
                sp.dma_start(out_rows[NCH - 1], r[(NCH - 1) % 2][:]).then_inc(S[f"out{(NCH - 1) % 2}"], 16)
                for i in range(2):
                    sp.wait_ge(S[f"out{i}"], 16 * ((NCH + 1 - i) // 2))

            @block.vector
            def _(dve):
                chain = Chain(dve, S["ch"], 6)
                for c in range(NCH):
                    chain.begin(c)
                    t = q[c % 2]
                    o = r[c % 2]
                    a = attr[:, c * CH:(c + 1) * CH]
                    k = keep[:, c * CH:(c + 1) * CH, :]
                    dve.wait_ge(S[f"x{c % 2}"], 16 * (c // 2) + 16)
                    chain.step(dve.tensor_scalar(f[:, 0, :], t[:, :, QW - 1], 1.0, None, ALU.max))
                    chain.step(dve.reciprocal(f[:, 1, :], f[:, 0, :]))
                    chain.step(dve.scalar_tensor_tensor(f[:, 2, :], f[:, 1, :], 1 / math.sqrt(96.0), a, ALU.mult, ALU.mult))
                    chain.step(dve.tensor_tensor(f[:, 3, :], f[:, 2, :], t[:, :, CS], ALU.mult))
                    chain.step(dve.tensor_tensor(f[:, 3, :], f[:, 3, :], f[:, 2, :], ALU.mult))
                    by = f[:, 3, :].unsqueeze(2)
                    dve.tensor_tensor(t[:, :, 0:CS], t[:, :, 0:CS], by.broadcast_to([P, CH, CS]), ALU.mult)
                    chain.step(dve.tensor_tensor(t[:, :, CS + 1:QW - 1], t[:, :, CS + 1:QW - 1], by.broadcast_to([P, CH, 96]), ALU.mult))
                    if c >= 2:
                        dve.wait_ge(S[f"out{c % 2}"], 16 * (c // 2))
                    dve.tensor_tensor(o[:, :, 0:CS], t[:, :, 0:CS], k[:, :, 0:CS], ALU.add)
                    for x in range(3):
                        last = dve.tensor_tensor(o[:, :, CS + x:D:3], t[:, :, CS + 1 + CV * x:CS + 1 + CV * x + CV], k[:, :, CS + x:D:3], ALU.add)
                    last.then_inc(S["res"], 1)
                    chain.end()


def kernel(**inputs):
    import concourse.bacc as bacc
    from concourse.bass_utils import run_bass_kernel_spmd

    a = {n: np.asarray(v) for n, v in inputs.items()}
    pad_e = NG_PAD * GE - N_EDGES
    src = np.pad(a["src"], (0, pad_e)).reshape(NG_PAD, TILES, P)
    dst = np.pad(a["dst"], (0, pad_e), constant_values=N_NODES).reshape(NG_PAD, TILES, P)
    y = np.pad(a["edge_attr_4"], ((0, pad_e), (0, 0)))
    arrays = {
        "x": np.pad(a["x"], ((0, NODES_PAD - N_NODES), (0, 0))),
        "node_attr": np.pad(a["node_vec1"][:, 0], (0, NODES_PAD - N_NODES)).reshape(NT, P).T,
        "idx": np.concatenate([src, dst], axis=1).transpose(0, 2, 1),
        "dst_rows": dst.reshape(NG_PAD, GE),
        "rbf": np.pad(a["edge_attr_16"], ((0, pad_e), (0, 0))).reshape(NG_PAD, GE, NB).transpose(0, 2, 1),
        "y": y.reshape(NG_PAD, GE, 4).transpose(0, 2, 1),
        "y_edge": y.reshape(NG_PAD, TILES, P, 4).transpose(0, 2, 1, 3),
        "Ws_val_t": a["L0_gnn_Ws_val"].T,
        "alpha_dot": a["L0_gnn_alpha_dot"].reshape(-1),
    }
    for n in ("gamma_s", "beta_s", "gamma_v", "Ws_src", "Wv_src", "Ws_dst", "Wv_dst", "W_rbf", "W_alpha", "Ws_val",
              "Wv_val", "Wg", "Ws_vlin", "Wv_vlin", "Wps", "Wpv"):
        arrays[n] = a["L0_gnn_" + n]
    for n in ("w2_ss", "w2_sv", "w2_vs", "w2_vv0", "w2_vv1"):
        arrays[n] = a["L0_gnn_" + n].reshape(-1, 1)
    for n in ("Wfc1", "Wfc2", "Wsc0", "Wsc1", "Wl1_0", "Wl1_1", "Wl2_s", "Wl2_v", "Wa"):
        arrays[n] = a["L1_gnn_" + n]
    arrays = {"in_" + n: np.ascontiguousarray(v) for n, v in arrays.items()}
    nc = bacc.Bacc("TRN2", target_bir_lowering=False, num_devices=1)
    ins = {n[3:]: nc.dram_tensor(n, v.shape, mybir.dt.from_np(v.dtype), kind="ExternalInput").ap() for n, v in arrays.items()}
    out = nc.dram_tensor("out", (NODES_PAD, D), F32, kind="ExternalOutput").ap()
    build(nc, ins, out)
    return run_bass_kernel_spmd(nc, [arrays], core_ids=[0]).results[0]["out"][:N_NODES]
```
